# Optimizing a Trainium2 kernel written in Bass

```python
import numpy as np
import jax
import jax.numpy as jnp

def _softmax(x, axis=-1):
    return jax.nn.softmax(x, axis=axis)

def _gelu(x):
    return jax.nn.gelu(x, approximate=True)

def _silu(x):
    return jax.nn.silu(x)

def _sigmoid(x):
    return jax.nn.sigmoid(x)

def _layernorm(x, axis=-1, eps=1e-05):
    m = jnp.mean(x, axis=axis, keepdims=True)
    v = jnp.var(x, axis=axis, keepdims=True)
    return (x - m) / jnp.sqrt(v + eps)

def _scatter_add(tgt, idx, src, axis=0):
    return tgt.at[idx].add(src)

def _segment_sum(src, seg, n):
    return jax.ops.segment_sum(src, seg, n)
kernel_name = 'mk_vit_tower_d1_tok_img512_r4_52572f'

def setup_inputs(seed: int=0):
    np.random.seed(seed)
    _w = jnp.asarray

    def _rec_inputs():
        import jax
        import jax.numpy as jnp
        _rk = jax.random.key(seed)
        x = -0.000147625 + 0.999875 * jax.random.normal(jax.random.fold_in(_rk, 1), (64, 3, 224, 224), jnp.float32)
        return x
    x = _rec_inputs()

    def _L0_tok_setup():
        import jax, jax.numpy as jnp
        import numpy as np
        N_PATCHES = 8
        PATCH = 28
        C = 3
        IN_D = C * PATCH * PATCH
        HID = 128
        SEQ = N_PATCHES * N_PATCHES + 1

        def _positional_embedding(seq_len, dim):
            i = np.arange(seq_len)[:, None].astype(np.float32)
            j = np.arange(dim)[None, :].astype(np.float32)
            ang = i / np.power(100000.0, j / dim)
            pe = np.where(j % 2 == 0, np.sin(ang), np.cos(ang))
            return jnp.asarray(pe, dtype=jnp.float32)
        key = jax.random.key(seed)
        k1, k2, k3, k4 = jax.random.split(key, 4)
        B = 64
        X = jax.random.normal(k1, (B, C, 224, 224), dtype=jnp.float32)
        bound = 1.0 / np.sqrt(IN_D)
        W = jax.random.uniform(k2, (HID, IN_D), minval=-bound, maxval=bound, dtype=jnp.float32)
        b = jax.random.uniform(k3, (HID,), minval=-bound, maxval=bound, dtype=jnp.float32)
        class_token = jax.random.uniform(k4, (1, HID), dtype=jnp.float32)
        pos_embed = _positional_embedding(SEQ, HID)
        return {'X': X, 'W': W, 'b': b, 'class_token': class_token, 'pos_embed': pos_embed}
    _L0_tok_all = _L0_tok_setup()
    _L0_tok_in = {k: v for k, v in _L0_tok_all.items() if k in ('W', 'b', 'class_token', 'pos_embed')}
    del _L0_tok_all

    def _L0_attn_setup():
        import jax, jax.numpy as jnp
        import numpy as np
        L = 4
        D_MODEL = 128
        D_INNER = 256
        D_STATE = 64
        D_CONV = 4
        BATCH = 64
        SEQ = 117

        def _layer_norm(v, g, b, eps=1e-05):
            mu = v.mean(-1, keepdims=True)
            var = ((v - mu) ** 2).mean(-1, keepdims=True)
            return (v - mu) / jnp.sqrt(var + eps) * g + b

        def _mamba_block(x, in_w, cw, cb, xw, dw, db, alog, dvec, ow, g, b):
            xz = x @ in_w
            xm, z = jnp.split(xz, 2, axis=-1)
            lhs = xm.transpose(0, 2, 1)
            conv = jax.lax.conv_general_dilated(lhs, cw, window_strides=(1,), padding=[(D_CONV - 1, 0)], dimension_numbers=('NCH', 'OIH', 'NCH'), feature_group_count=D_INNER)
            xc = jax.nn.silu(conv.transpose(0, 2, 1) + cb)
            Bp, Cp = jnp.split(xc @ xw, 2, axis=-1)
            dt = jax.nn.softplus(xc @ dw + db)
            A = -jnp.exp(alog)

            def step(h, inp):
                xt, dtt, Bt, Ct = inp
                h = jnp.exp(dtt[..., None] * A) * h + (dtt * xt)[..., None] * Bt[:, None, :]
                y = jnp.einsum('bdn,bn->bd', h, Ct) + dvec * xt
                return (h, y)
            h0 = jnp.zeros((x.shape[0], D_INNER, D_STATE), x.dtype)
            xs = (xc.transpose(1, 0, 2), dt.transpose(1, 0, 2), Bp.transpose(1, 0, 2), Cp.transpose(1, 0, 2))
            _, ys = jax.lax.scan(step, h0, xs)
            y = ys.transpose(1, 0, 2) * jax.nn.silu(z)
            out = y @ ow
            return _layer_norm(out + x, g, b)
        key = jax.random.key(seed)
        ks = jax.random.split(key, 7)
        s = 0.02
        x = jax.random.normal(ks[0], (BATCH, SEQ, D_MODEL), jnp.float32)
        in_proj_w = jax.random.normal(ks[1], (L, D_MODEL, 2 * D_INNER), jnp.float32) * s
        conv_w = jax.random.normal(ks[2], (L, D_INNER, 1, D_CONV), jnp.float32) * s
        conv_b = jnp.zeros((L, D_INNER), jnp.float32)
        x_proj_w = jax.random.normal(ks[3], (L, D_INNER, 2 * D_STATE), jnp.float32) * s
        dt_w = jax.random.normal(ks[4], (L, D_INNER, D_INNER), jnp.float32) * s
        dt_b = jnp.full((L, D_INNER), -1.0, jnp.float32)
        A_log = jnp.tile(jnp.log(jnp.arange(1.0, D_STATE + 1, dtype=jnp.float32)), (L, D_INNER, 1))
        D_param = jnp.ones((L, D_INNER), jnp.float32)
        out_w = jax.random.normal(ks[5], (L, D_INNER, D_MODEL), jnp.float32) * s
        ln_g = jnp.ones((L, D_MODEL), jnp.float32)
        ln_b = jnp.zeros((L, D_MODEL), jnp.float32)
        return {'x': x, 'in_proj_w': in_proj_w, 'conv_w': conv_w, 'conv_b': conv_b, 'x_proj_w': x_proj_w, 'dt_w': dt_w, 'dt_b': dt_b, 'A_log': A_log, 'D_param': D_param, 'out_w': out_w, 'ln_g': ln_g, 'ln_b': ln_b}
    _L0_attn_all = _L0_attn_setup()
    _L0_attn_in = {k: v for k, v in _L0_attn_all.items() if k in ('in_proj_w', 'conv_w', 'conv_b', 'x_proj_w', 'dt_w', 'dt_b', 'A_log', 'D_param', 'out_w', 'ln_g', 'ln_b')}
    del _L0_attn_all

    def _L0_ffn_setup():
        import jax, jax.numpy as jnp
        import numpy as np
        B, N, DIM = (1, 512, 128)
        DH, H = (64, 8)
        E, FF = (8, 512)

        def _layernorm(x, g, b, eps=1e-05):
            mu = jnp.mean(x, axis=-1, keepdims=True)
            var = jnp.mean(jnp.square(x - mu), axis=-1, keepdims=True)
            return (x - mu) * jax.lax.rsqrt(var + eps) * g + b

        def _l2norm(x, eps=1e-12):
            return x / jnp.sqrt(jnp.sum(jnp.square(x), axis=-1, keepdims=True) + eps)
        key = jax.random.key(seed)
        ks = jax.random.split(key, 12)
        g = lambda k, shape: jax.random.normal(k, shape, jnp.float32) * 0.02
        return {'x': jax.random.normal(ks[0], (B, N, DIM), jnp.float32), 'ln_g': jnp.ones((DIM,), jnp.float32), 'ln_b': jnp.zeros((DIM,), jnp.float32), 'Wq': g(ks[1], (DIM, DIM)), 'Wk': g(ks[2], (DIM, DIM)), 'Wv': g(ks[3], (DIM, DIM)), 'Wo': g(ks[4], (DIM, DIM)), 'qn_g': jnp.ones((DH,), jnp.float32), 'kn_g': jnp.ones((DH,), jnp.float32), 'gate_W': g(ks[5], (DIM, E)), 'gate_b': jnp.zeros((E,), jnp.float32), 'W1': g(ks[6], (E, DIM, FF)), 'b1': jnp.zeros((E, FF), jnp.float32), 'W2': g(ks[7], (E, FF, DIM)), 'b2': jnp.zeros((E, DIM), jnp.float32)}
    _L0_ffn_all = _L0_ffn_setup()
    _L0_ffn_in = {k: v for k, v in _L0_ffn_all.items() if k in ('ln_g', 'ln_b', 'Wq', 'Wk', 'Wv', 'Wo', 'qn_g', 'kn_g', 'gate_W', 'gate_b', 'W1', 'b1', 'W2', 'b2')}
    del _L0_ffn_all
    return {'x': x, 'L0_tok_W': _L0_tok_in['W'], 'L0_tok_b': _L0_tok_in['b'], 'L0_tok_class_token': _L0_tok_in['class_token'], 'L0_tok_pos_embed': _L0_tok_in['pos_embed'], 'L0_attn_in_proj_w': _L0_attn_in['in_proj_w'], 'L0_attn_conv_w': _L0_attn_in['conv_w'], 'L0_attn_conv_b': _L0_attn_in['conv_b'], 'L0_attn_x_proj_w': _L0_attn_in['x_proj_w'], 'L0_attn_dt_w': _L0_attn_in['dt_w'], 'L0_attn_dt_b': _L0_attn_in['dt_b'], 'L0_attn_A_log': _L0_attn_in['A_log'], 'L0_attn_D_param': _L0_attn_in['D_param'], 'L0_attn_out_w': _L0_attn_in['out_w'], 'L0_attn_ln_g': _L0_attn_in['ln_g'], 'L0_attn_ln_b': _L0_attn_in['ln_b'], 'L0_ffn_ln_g': _L0_ffn_in['ln_g'], 'L0_ffn_ln_b': _L0_ffn_in['ln_b'], 'L0_ffn_Wq': _L0_ffn_in['Wq'], 'L0_ffn_Wk': _L0_ffn_in['Wk'], 'L0_ffn_Wv': _L0_ffn_in['Wv'], 'L0_ffn_Wo': _L0_ffn_in['Wo'], 'L0_ffn_qn_g': _L0_ffn_in['qn_g'], 'L0_ffn_kn_g': _L0_ffn_in['kn_g'], 'L0_ffn_gate_W': _L0_ffn_in['gate_W'], 'L0_ffn_gate_b': _L0_ffn_in['gate_b'], 'L0_ffn_W1': _L0_ffn_in['W1'], 'L0_ffn_b1': _L0_ffn_in['b1'], 'L0_ffn_W2': _L0_ffn_in['W2'], 'L0_ffn_b2': _L0_ffn_in['b2']}

def reference(x, L0_tok_W, L0_tok_b, L0_tok_class_token, L0_tok_pos_embed, L0_attn_in_proj_w, L0_attn_conv_w, L0_attn_conv_b, L0_attn_x_proj_w, L0_attn_dt_w, L0_attn_dt_b, L0_attn_A_log, L0_attn_D_param, L0_attn_out_w, L0_attn_ln_g, L0_attn_ln_b, L0_ffn_ln_g, L0_ffn_ln_b, L0_ffn_Wq, L0_ffn_Wk, L0_ffn_Wv, L0_ffn_Wo, L0_ffn_qn_g, L0_ffn_kn_g, L0_ffn_gate_W, L0_ffn_gate_b, L0_ffn_W1, L0_ffn_b1, L0_ffn_W2, L0_ffn_b2):
    import jax
    import jax.numpy as jnp

    def _L0_tok_ref(X, W, b, class_token, pos_embed):
        import jax, jax.numpy as jnp
        import numpy as np
        N_PATCHES = 8
        PATCH = 28
        C = 3
        IN_D = C * PATCH * PATCH
        HID = 128
        SEQ = N_PATCHES * N_PATCHES + 1

        def _positional_embedding(seq_len, dim):
            i = np.arange(seq_len)[:, None].astype(np.float32)
            j = np.arange(dim)[None, :].astype(np.float32)
            ang = i / np.power(100000.0, j / dim)
            pe = np.where(j % 2 == 0, np.sin(ang), np.cos(ang))
            return jnp.asarray(pe, dtype=jnp.float32)
        B = X.shape[0]
        patches = X.reshape(B, C, N_PATCHES, PATCH, N_PATCHES, PATCH)
        patches = patches.transpose(0, 2, 4, 1, 3, 5).reshape(B, N_PATCHES * N_PATCHES, IN_D)
        tokens = jnp.einsum('bpi,hi->bph', patches, W) + b
        cls = jnp.broadcast_to(class_token[None, :, :], (B, 1, HID))
        tokens = jnp.concatenate([cls, tokens], axis=1)
        return tokens * pos_embed[None, :, :]

    def _L0_attn_ref(x, in_proj_w, conv_w, conv_b, x_proj_w, dt_w, dt_b, A_log, D_param, out_w, ln_g, ln_b):
        import jax, jax.numpy as jnp
        import numpy as np
        L = 4
        D_MODEL = 128
        D_INNER = 256
        D_STATE = 64
        D_CONV = 4
        BATCH = 64
        SEQ = 117

        def _layer_norm(v, g, b, eps=1e-05):
            mu = v.mean(-1, keepdims=True)
            var = ((v - mu) ** 2).mean(-1, keepdims=True)
            return (v - mu) / jnp.sqrt(var + eps) * g + b

        def _mamba_block(x, in_w, cw, cb, xw, dw, db, alog, dvec, ow, g, b):
            xz = x @ in_w
            xm, z = jnp.split(xz, 2, axis=-1)
            lhs = xm.transpose(0, 2, 1)
            conv = jax.lax.conv_general_dilated(lhs, cw, window_strides=(1,), padding=[(D_CONV - 1, 0)], dimension_numbers=('NCH', 'OIH', 'NCH'), feature_group_count=D_INNER)
            xc = jax.nn.silu(conv.transpose(0, 2, 1) + cb)
            Bp, Cp = jnp.split(xc @ xw, 2, axis=-1)
            dt = jax.nn.softplus(xc @ dw + db)
            A = -jnp.exp(alog)

            def step(h, inp):
                xt, dtt, Bt, Ct = inp
                h = jnp.exp(dtt[..., None] * A) * h + (dtt * xt)[..., None] * Bt[:, None, :]
                y = jnp.einsum('bdn,bn->bd', h, Ct) + dvec * xt
                return (h, y)
            h0 = jnp.zeros((x.shape[0], D_INNER, D_STATE), x.dtype)
            xs = (xc.transpose(1, 0, 2), dt.transpose(1, 0, 2), Bp.transpose(1, 0, 2), Cp.transpose(1, 0, 2))
            _, ys = jax.lax.scan(step, h0, xs)
            y = ys.transpose(1, 0, 2) * jax.nn.silu(z)
            out = y @ ow
            return _layer_norm(out + x, g, b)
        for i in range(L):
            x = _mamba_block(x, in_proj_w[i], conv_w[i], conv_b[i], x_proj_w[i], dt_w[i], dt_b[i], A_log[i], D_param[i], out_w[i], ln_g[i], ln_b[i])
        return x

    def _L0_ffn_ref(x, ln_g, ln_b, Wq, Wk, Wv, Wo, qn_g, kn_g, gate_W, gate_b, W1, b1, W2, b2):
        import jax, jax.numpy as jnp
        import numpy as np
        B, N, DIM = (1, 512, 128)
        DH, H = (64, 8)
        E, FF = (8, 512)

        def _layernorm(x, g, b, eps=1e-05):
            mu = jnp.mean(x, axis=-1, keepdims=True)
            var = jnp.mean(jnp.square(x - mu), axis=-1, keepdims=True)
            return (x - mu) * jax.lax.rsqrt(var + eps) * g + b

        def _l2norm(x, eps=1e-12):
            return x / jnp.sqrt(jnp.sum(jnp.square(x), axis=-1, keepdims=True) + eps)
        b, n, d = x.shape
        dh = qn_g.shape[0]
        h = d // dh
        hx = _layernorm(x, ln_g, ln_b)
        q = (hx @ Wq).reshape(b, n, h, dh).transpose(0, 2, 1, 3)
        k = (hx @ Wk).reshape(b, n, h, dh).transpose(0, 2, 1, 3)
        v = (hx @ Wv).reshape(b, n, h, dh).transpose(0, 2, 1, 3)
        scale = jnp.sqrt(jnp.float32(dh))
        q = _l2norm(q) * scale * qn_g
        k = _l2norm(k) * scale * kn_g
        scores = jnp.einsum('bhqd,bhkd->bhqk', q, k) * dh ** (-0.5)
        causal = jnp.tril(jnp.ones((n, n), bool))
        scores = jnp.where(causal, scores, jnp.finfo(scores.dtype).min)
        attn = jax.nn.softmax(scores, axis=-1)
        o = jnp.einsum('bhqk,bhkd->bhqd', attn, v)
        y = o.transpose(0, 2, 1, 3).reshape(b, n, d) @ Wo
        gate = jax.nn.softmax(y @ gate_W + gate_b, axis=-1)
        hid = jax.nn.gelu(jnp.einsum('bnd,edf->bnef', y, W1) + b1)
        eo = jnp.einsum('bnef,efd->bned', hid, W2) + b2
        out = jnp.einsum('bned,bne->bnd', eo, gate)
        return out
    h = _L0_tok_ref(x, L0_tok_W, L0_tok_b, L0_tok_class_token, L0_tok_pos_embed)
    h = h + _L0_attn_ref(_layernorm(h, axis=-1), L0_attn_in_proj_w, L0_attn_conv_w, L0_attn_conv_b, L0_attn_x_proj_w, L0_attn_dt_w, L0_attn_dt_b, L0_attn_A_log, L0_attn_D_param, L0_attn_out_w, L0_attn_ln_g, L0_attn_ln_b)
    h = h + _L0_ffn_ref(_layernorm(h, axis=-1), L0_ffn_ln_g, L0_ffn_ln_b, L0_ffn_Wq, L0_ffn_Wk, L0_ffn_Wv, L0_ffn_Wo, L0_ffn_qn_g, L0_ffn_kn_g, L0_ffn_gate_W, L0_ffn_gate_b, L0_ffn_W1, L0_ffn_b1, L0_ffn_W2, L0_ffn_b2)
    return h

_drawn_inputs = setup_inputs


def setup_inputs(seed=0):
    import zlib

    import numpy as np

    out = dict(_drawn_inputs(seed))
    spreads = {'L0_attn_conv_b': (0.0, 0.8),
     'L0_attn_dt_b': (-1.0, 0.6),
     'L0_attn_D_param': (1.0, 0.6),
     'L0_attn_ln_g': (1.0, 0.2),
     'L0_attn_ln_b': (0.0, 0.1),
     'L0_ffn_ln_g': (1.0, 0.6),
     'L0_ffn_ln_b': (0.0, 0.8),
     'L0_ffn_qn_g': (1.0, 0.6),
     'L0_ffn_kn_g': (1.0, 0.6),
     'L0_ffn_gate_b': (0.0, 0.8),
     'L0_ffn_b1': (0.0, 0.8),
     'L0_ffn_b2': (0.0, 1.338)}
    factors = {'L0_attn_in_proj_w': 8.0,
     'L0_attn_conv_w': 8.0,
     'L0_attn_x_proj_w': 8.0,
     'L0_attn_dt_w': 8.0,
     'L0_attn_A_log': 8.0,
     'L0_attn_out_w': 8.0,
     'L0_ffn_Wq': 8.0,
     'L0_ffn_Wk': 8.0,
     'L0_ffn_Wv': 8.0,
     'L0_ffn_Wo': 8.0,
     'L0_ffn_gate_W': 8.0,
     'L0_ffn_W1': 8.0,
     'L0_ffn_W2': 8.0}
    for name, (base, spread) in spreads.items():
        noise = np.random.default_rng([zlib.crc32(name.encode()), seed]).standard_normal(out[name].shape)
        drawn = base * np.exp(spread * noise) if base else spread * noise
        out[name] = jnp.asarray(drawn.astype(out[name].dtype))
    for name, factor in factors.items():
        out[name] = (out[name] * factor).astype(out[name].dtype)
    return out
```

```python
from contextlib import ExitStack

import numpy as np

import concourse.bass as bass
from concourse import mybir

ALU = mybir.AluOpType
ACT = mybir.ActivationFunctionType
AX_X = mybir.AxisListType.X
F32 = mybir.dt.float32
BF16 = mybir.dt.bfloat16
ds = bass.ds

B, C, IMG, PATCH, GRID = 64, 3, 224, 28, 8
SEQ = GRID * GRID + 1
D = 128
DI = 256
NST = 64
LAYERS = 4
TAPS = 4
E, FF = 8, 512
FB = FF // 128
HEADS, DH = 2, 64
HALVES = 2
HB = B // HALVES
T = HB * SEQ
NP = 5
PW = T // NP
ROWS = C * PATCH
TOKB = 4
TOKG = HB // TOKB
TOKE = TOKB * GRID * IMG
AB = 4
AG = HB // AB
AW = AB * SEQ
MB = 4
MT = PW // MB
NPAR = 2 * TAPS + 2 + 2 + 2 + 1 + 1 + 2 * NST
GSTEP = NST // 2
EPS = 1e-5
LN_PER_HALF = LAYERS + 3


def bass_vit_tower(nc, x, w_tok, v_tok, pos, w_in, w_x, w_dt, w_out, par, w_att, w_gate, v_ffn, r_ffn, w1, w2,
                   consts, onehot, mask, out):
    with ExitStack() as ctx:
        def sb(name, shape, dt=F32):
            return ctx.enter_context(nc.sbuf_tensor(name, shape, dt))

        def sem(name):
            return ctx.enter_context(nc.semaphore(name))

        ps = ctx.enter_context(nc.psum_tensor("ps", [128, 8, 512], F32))

        h0 = sb("h0", [128, T])
        xs = sb("xs", [128, T])
        arena = sb("arena", [128, 4 * 2 * T])
        xc, dt, dtx, z = (arena[:, k * 2 * T:(k + 1) * 2 * T] for k in range(4))
        patch = [arena[0:ROWS, u * TOKE:(u + 1) * TOKE] for u in range(2)]
        abuf = [sb(f"decay{u}", [128, T]) for u in range(2)]
        bbuf = [sb(f"drive{v}", [128, T]) for v in range(4)]
        hbuf = [sb(f"state{u}", [128, T]) for u in range(2)]
        part = [bbuf[1 + k][:].bitcast(BF16)[:, 0:T] for k in range(3)]
        stack = sb("stack", [96, 4, T], BF16)
        sel = sb("sel", [96, GSTEP, 128], BF16)
        eye32 = sb("eye32", [96, GSTEP])
        wtok = sb("wtok", [ROWS, PATCH * D])
        lw = sb("lw", [128, 2 * DI + 2 * D + 2 * DI + 2 * D])
        pk = sb("pk", [128, NPAR])
        nega = sb("nega", [128, 2 * NST])
        dskip = sb("dskip", [128, 2, 128])
        cst = sb("cst", [128, 3 * 128])
        msk = sb("msk", [SEQ, SEQ])
        vtok = sb("vtok", [128, 2])
        posT = sb("posT", [128, SEQ])
        watt = sb("watt", [128, 4 * D])
        wgate = sb("wgate", [128, E])
        vffn = sb("vffn", [128, 4 + E * FB])
        rffn = sb("rffn", [1, E + E * D + 128])
        eps = sb("eps", [128, 2])
        kg8 = sb("kg8", [128, 1])
        small = sb("small", [128, 64])

        ident, mean_w, head_w = (cst[:, k * 128:(k + 1) * 128] for k in range(3))
        inw = lw[:, 0:2 * DI]
        xw = lw[:, 512:768].rearrange("p (k m) -> p k m", k=2)
        dw = lw[:, 768:1280].rearrange("p (k m) -> p k m", k=2)
        ow = lw[:, 1280:1536].rearrange("p (k m) -> p k m", k=2)
        conv_w = pk[:, 0:2 * TAPS].rearrange("p (h k) -> p h k", h=2)
        conv_b, dt_b, dvec = pk[:, 8:10], pk[:, 10:12], pk[:, 12:14]
        ln_g, ln_b = pk[:, 14:15], pk[:, 15:16]
        alog = pk[:, 16:16 + 2 * NST]
        gate_b, b2row, ones = rffn[:, 0:E], rffn[:, E:E + E * D], rffn[:, E + E * D:]

        const_ld = sem("const_ld")
        sel_made = sem("sel_made")
        par_ld, par_used = sem("par_ld"), sem("par_used")
        patch_ld = [sem("patch_ld0"), sem("patch_ld1")]
        tok_mm, tok_ev, cls_done = sem("tok_mm"), sem("tok_ev"), sem("cls_done")
        ln_mean, ln_cen, ln_sq, ln_var = sem("ln_mean"), sem("ln_cen"), sem("ln_sq"), sem("ln_var")
        ln_log, ln_rstd, ln_nrm, ln_out = sem("ln_log"), sem("ln_rstd"), sem("ln_nrm"), sem("ln_out")
        proj_mm, proj_ev = sem("proj_mm"), sem("proj_ev")
        conv_step, conv_done, xc_ready = sem("conv_step"), sem("conv_done"), sem("xc_ready")
        bc_mm, hi_done, r1_done, mid_done, lo_done = (sem(n) for n in ("bc_mm", "hi_done", "r1_done", "mid_done", "lo_done"))
        stacked = sem("stacked")
        dt_mm, dt_abs, dt_relu, dt_exp, dt_log = (sem(n) for n in ("dt_mm", "dt_abs", "dt_relu", "dt_exp", "dt_log"))
        dt_ready, dtx_ready = sem("dt_ready"), sem("dtx_ready")
        aexp_done, nega_ready, dskip_ready = sem("aexp_done"), sem("nega_ready"), sem("dskip_ready")
        edge_zero = sem("edge_zero")
        b_spread, b_moved = sem("b_spread"), sem("b_moved")
        c_spread, g_ready = sem("c_spread"), sem("g_ready")
        a_ready, b_ready = sem("a_ready"), sem("b_ready")
        scanned, y_added = sem("scanned"), sem("y_added")
        y_sum, y_gated = sem("y_sum"), sem("y_gated")
        o_mm, o_res = sem("o_mm"), sem("o_res")
        h1_ready = sem("h1_ready")
        expw_ld = sem("expw_ld")
        att = {n: sem("att_" + n) for n in ("hg", "qkv", "sq", "ssq", "log", "r", "n", "s", "soft", "sub", "e", "p",
                                            "t", "pt", "o", "oc", "y", "yc")}
        kg_done = sem("kg_done")
        cp_done, tr_mm, gate_mm = sem("cp_done"), sem("tr_mm"), sem("gate_mm")
        g_soft, g_sub, g_exp = sem("g_soft"), sem("g_sub"), sem("g_exp")
        hid_mm, hid_done = sem("hid_mm"), sem("hid_done")
        exp_mm, exp_added = sem("exp_mm"), sem("exp_added")
        acc_step = sem("acc_step")
        piece_done = sem("piece_done")
        out_st = sem("out_st")

        def piece(ap, p):
            return ap[:, p * PW:(p + 1) * PW]

        def blk(ap, h):
            return ap[:, h * T:(h + 1) * T]

        def images(ap):
            return ap.rearrange("p (b t) -> p b t", t=SEQ)

        yT = xc[:, 0:T]
        hg = bbuf[0][:, 0:AW]
        sqk = bbuf[0][:, AW:3 * AW].rearrange("p (a t) -> p a t", a=2)
        rqk = bbuf[0][:, 3 * AW:5 * AW].rearrange("p (a t) -> p a t", a=2)
        qn, kn = bbuf[0][:, 5 * AW:6 * AW], bbuf[0][:, 6 * AW:7 * AW]
        osb = bbuf[0][:, 7 * AW:8 * AW]
        vsb = bbuf[1][0:SEQ, 0:512].rearrange("p (b d) -> p b d", b=AB)
        sc = bbuf[1][0:SEQ, 512:512 + 8 * SEQ]
        pT = bbuf[1][0:SEQ, 1040:1040 + 8 * SEQ].rearrange("p (h b t) -> p h b t", h=HEADS, b=AB)
        yp, hp = hbuf[0][:, 0:PW], hbuf[0][:, PW:2 * PW]
        acc = hbuf[0][0:MT, 2 * PW:2 * PW + MB * D]
        lg = hbuf[1][0:MT, 0:MB * E]
        gate = hbuf[1][0:MT, 64:64 + MB * E]
        hid = [z[:, u * FB * PW:(u + 1) * FB * PW] for u in range(2)]
        w1s = dt[:, 0:E * FF]
        w2s = dtx[:, 0:E * FB * D].rearrange("p (e f d) -> p e f d", e=E, f=FB)

        block = ctx.enter_context(nc.Block())

        @block.sync
        def _(sp):
            for dst, src in ((wtok[:], w_tok), (vtok[:], v_tok), (posT[:], pos), (cst[:], consts),
                             (eye32[:], onehot), (msk[:], mask), (watt[:], w_att), (wgate[:], w_gate),
                             (vffn[:], v_ffn), (rffn[:], r_ffn)):
                sp.dma_start(dst, src).then_inc(const_ld, 16)
            sp.sem_inc(out_st, 16)
            with sp.Fori(0, HALVES) as hf:
                with sp.Fori(0, TOKG // 2) as j:
                    for u in range(2):
                        g = hf * TOKG + j * 2 + u
                        group = sp.snap(g * TOKE)
                        sp.wait_ge(tok_mm, hf * (TOKG + 2) + j * 2 + u + 1)
                        sp.dma_start(patch[u], x[:, ds(group, TOKE)]).then_inc(patch_ld[u], 16)
                with sp.Fori(0, LAYERS) as layer:
                    R = hf * LAYERS + layer
                    layer = sp.snap(layer)
                    sp.wait_ge(par_used, R + 1)
                    for dst, src in ((inw, w_in[ds(layer, 1)].rearrange("o p m -> (o p) m")),
                                     (xw, w_x[ds(layer, 1)].rearrange("o (k p) m -> p (o k) m", p=128)),
                                     (dw, w_dt[ds(layer, 1)].rearrange("o (k p) m -> p (o k) m", p=128)),
                                     (ow, w_out[ds(layer, 1)].rearrange("o (k p) m -> p (o k) m", p=128)),
                                     (pk[:], par[ds(layer, 1)].rearrange("o p m -> (o p) m"))):
                        sp.dma_start(dst, src).then_inc(par_ld, 16)
                    for k, ready in enumerate((hi_done, mid_done, lo_done)):
                        sp.wait_ge(ready, R * NP + NP)
                        for grp in range(4):
                            sp.dma_start(stack[32 * k:32 * k + 32, grp, :],
                                         part[k][32 * grp:32 * grp + 32, :]).then_inc(stacked, 16)
                sp.wait_ge(h1_ready, hf + 1)
                sp.dma_start(w1s, w1).then_inc(expw_ld, 16)
                sp.dma_start(w2s.rearrange("p e f d -> p (e f d)"), w2).then_inc(expw_ld, 16)
                with sp.Fori(0, NP) as p:
                    q = hf * NP + p
                    row = sp.snap(q * PW)
                    sp.wait_ge(piece_done, q + 2)
                    sp.dma_start(out[ds(row, PW)].rearrange("(t p) d -> p t d", p=MT),
                                 acc.rearrange("p (t d) -> p t d", t=MB)).then_inc(out_st, 16)
            sp.wait_ge(out_st, 16 * (HALVES * NP + 1))

        @block.tensor
        def _(pe):
            def norm(inst, source, src_ready, src_count):
                for p in range(NP):
                    pe.wait_ge(src_ready, src_count[p])
                    nc.tensor.matmul(ps[:, p, 0:PW], mean_w, piece(source, p), start=True, stop=True).then_inc(ln_mean, 1)
                for p in range(NP):
                    pe.wait_ge(ln_sq, inst * NP + p + 1)
                    if p >= 3:
                        pe.wait_ge(ln_log, inst * NP + p - 2)
                    nc.tensor.matmul(ps[:, NP + p % 3, 0:PW], mean_w, piece(bbuf[1], p), start=True,
                                     stop=True).then_inc(ln_var, 1)

            pe.sem_inc(y_added, 2)
            pe.sem_inc(exp_mm, 2)
            pe.sem_inc(par_used, 1)
            pe.wait_ge(const_ld, 160)
            pe.wait_ge(sel_made, 1)
            with pe.Fori(0, HALVES) as hf:
                with pe.Fori(0, TOKG // 2) as j:
                    for u in range(2):
                        g = hf * TOKG + j * 2 + u
                        pe.wait_ge(patch_ld[u], (hf * (TOKG // 2) + j) * 16 + 16)
                        pe.wait_ge(tok_ev, g + 1)
                        for k in range(PATCH):
                            mm = nc.tensor.matmul(
                                ps[:, u, 0:TOKB * 64], wtok[:, k * D:(k + 1) * D],
                                patch[u][:, k * TOKB * 64:(k + 1) * TOKB * 64], start=(k == 0), stop=(k == PATCH - 1))
                        mm.then_inc(tok_mm, 1)
                pe.wait_ge(cls_done, hf + 1)
                norm(hf * LN_PER_HALF, h0, tok_ev, [(hf + 1) * TOKG + 2] * NP)

                with pe.Fori(0, LAYERS) as layer:
                    R = hf * LAYERS + layer
                    pe.wait_ge(par_ld, R * 80 + 80)
                    for q in range(4 * NP):
                        if q < NP:
                            pe.wait_ge(ln_out, (hf * LN_PER_HALF + layer) * NP + NP)
                        if q >= 8:
                            pe.wait_ge(proj_ev, R * 4 * NP + q - 7)
                        nc.tensor.matmul(ps[:, q % 8, 0:PW], inw[:, (q // NP) * 128:(q // NP + 1) * 128],
                                         piece(xs, q % NP), start=True, stop=True).then_inc(proj_mm, 1)
                    pe.wait_ge(xc_ready, R * 2 + 2)
                    for p in range(NP):
                        for k in range(2):
                            mm = nc.tensor.matmul(ps[:, p, 0:PW], xw[:, k, :], piece(blk(xc, k), p), start=(k == 0),
                                                  stop=(k == 1))
                        mm.then_inc(bc_mm, 1)
                    for q in range(2 * NP):
                        bank = (NP + q) % 8
                        if 3 <= q < 8:
                            pe.wait_ge(r1_done, R * NP + q - 2)
                        if q >= 8:
                            pe.wait_ge(dt_relu, R * 2 * NP + q - 7)
                        for k in range(2):
                            mm = nc.tensor.matmul(ps[:, bank, 0:PW], dw[:, k, (q // NP) * 128:(q // NP + 1) * 128],
                                                  piece(blk(xc, k), q % NP), start=(k == 0), stop=(k == 1))
                        mm.then_inc(dt_mm, 1)
                    pe.wait_ge(dskip_ready, R + 1)
                    pe.wait_ge(dt_ready, R * 2 + 2)
                    pe.wait_ge(stacked, R * 192 + 192)
                    for h in range(2):
                        H = R * 2 + h
                        pe.wait_ge(y_gated, H + 1)

                        def spread_b(i, u, j, p):
                            pe.wait_ge(b_moved, (H * NST + i) * NP + p + 1)
                            nc.tensor.matmul(ps[:, 5, 0:PW], sel_row(j), stack[:, u, p * PW:(p + 1) * PW],
                                             start=True, stop=True).then_inc(b_spread, 1)

                        def spread_c(i, u, j, p):
                            pe.wait_ge(g_ready, (H * NST + i) * NP + p + 1)
                            nc.tensor.matmul(ps[:, 6 + (u + p) % 2, 0:PW], sel_row(j),
                                             stack[:, 2 + u, p * PW:(p + 1) * PW],
                                             start=True, stop=True).then_inc(c_spread, 1)

                        def step(j, u, first=False, last=False):
                            i = 2 * j + u
                            spread_c(i, u, j, 0)
                            spread_c(i, u, j, 1)
                            for p in range(NP):
                                if not last:
                                    spread_b(i + 2, u, j + 1, p)
                                if not first:
                                    add_y(i - 1, 1 - u, p)
                                if p == 3:
                                    spread_c(i, u, j, 2)
                            spread_c(i, u, j, 3)
                            spread_c(i, u, j, 4)

                        def add_y(i, u, p, last=False):
                            pe.wait_ge(g_ready, (H * NST + i) * NP + p + 3)
                            mm = nc.tensor.matmul(ps[:, p, 0:PW], ident, piece(hbuf[u], p), start=False,
                                                  stop=last, skip_group_check=True)
                            if p == NP - 1:
                                mm.then_inc(y_added, 1)

                        def sel_row(j):
                            return sel[:, ds(j, 1), :].rearrange("p o m -> p (o m)")

                        for p in range(NP):
                            nc.tensor.matmul(ps[:, p, 0:PW], dskip[:, h, :], piece(blk(xc, h), p), start=True,
                                             stop=False, skip_group_check=True)
                        for u in range(2):
                            for p in range(NP):
                                spread_b(u, u, 0, p)
                        step(0, 0, first=True)
                        step(0, 1)
                        with pe.Fori(1, GSTEP - 1) as j:
                            step(j, 0)
                            step(j, 1)
                        step(GSTEP - 1, 0, last=True)
                        step(GSTEP - 1, 1, last=True)
                        for p in range(NP):
                            add_y(NST - 1, 1, p, last=True)
                        pe.wait_ge(y_added, (H + 1) * NST + 2)
                        pe.sem_inc(y_sum, 1)
                    for p in range(NP):
                        pe.wait_ge(y_gated, R * 2 + 3)
                        for k in range(2):
                            mm = nc.tensor.matmul(ps[:, p, 0:PW], ow[:, k, :], piece(blk(z, k), p), start=(k == 0),
                                                  stop=(k == 1))
                        mm.then_inc(o_mm, 1)
                    norm(hf * LN_PER_HALF + 1 + layer, hbuf[1], o_res, [R * NP + p + 1 for p in range(NP)])

                norm(hf * LN_PER_HALF + 1 + LAYERS, h0, h1_ready, [hf + 1] * NP)
                norm(hf * LN_PER_HALF + 2 + LAYERS, xs, ln_out,
                     [(hf * LN_PER_HALF + LAYERS + 1) * NP + p + 1 for p in range(NP)])

                with pe.Fori(0, AG) as j:
                    g = hf * AG + j
                    pe.wait_ge(att["hg"], g + 1)
                    for k in range(2):
                        nc.tensor.matmul(ps[:, k, 0:AW], watt[:, k * D:(k + 1) * D], hg, start=True, stop=True)
                    for b in range(AB):
                        mm = nc.tensor.matmul(ps[0:SEQ, 2, b * D:(b + 1) * D], hg[:, b * SEQ:(b + 1) * SEQ],
                                              watt[:, 2 * D:3 * D], start=True, stop=True)
                    mm.then_inc(att["qkv"], 1)
                    pe.wait_ge(att["sq"], g + 1)
                    for k in range(2):
                        mm = nc.tensor.matmul(ps[:, 3 + k, 0:AW], head_w, sqk[:, k, :], start=True, stop=True)
                    mm.then_inc(att["ssq"], 1)
                    pe.wait_ge(att["n"], g + 1)
                    for h in range(HEADS):
                        hd = slice(h * DH, (h + 1) * DH)
                        for b in range(AB):
                            tk = slice(b * SEQ, (b + 1) * SEQ)
                            mm = nc.tensor.matmul(ps[0:SEQ, 5 + h, tk], qn[hd, tk], kn[hd, tk], start=True, stop=True)
                    mm.then_inc(att["s"], 1)
                    pe.wait_ge(att["p"], g + 1)
                    for h in range(HEADS):
                        for b in range(AB):
                            k = h * AB + b
                            mm = nc.tensor.transpose(ps[0:SEQ, 3 + h, b * SEQ:(b + 1) * SEQ],
                                                     sc[:, k * SEQ:(k + 1) * SEQ], ident[0:SEQ, 0:SEQ])
                    mm.then_inc(att["t"], 1)
                    pe.wait_ge(att["pt"], g + 1)
                    for h in range(HEADS):
                        hd = slice(h * DH, (h + 1) * DH)
                        for b in range(AB):
                            mm = nc.tensor.matmul(ps[hd, 0, b * SEQ:(b + 1) * SEQ], vsb[:, b, hd], pT[:, h, b, :],
                                                  start=True, stop=True)
                    mm.then_inc(att["o"], 1)
                    pe.wait_ge(att["oc"], g + 1)
                    nc.tensor.matmul(ps[:, 1, 0:AW], watt[:, 3 * D:4 * D], osb, start=True,
                                     stop=True).then_inc(att["y"], 1)

                with pe.Fori(0, NP) as p:
                    q = hf * NP + p
                    pe.wait_ge(expw_ld, hf * 32 + 32)
                    pe.wait_ge(cp_done, q * 2 + 2)
                    for t in range(MB):
                        mm = nc.tensor.transpose(ps[0:MT, 7, t * D:(t + 1) * D], hp[:, t * MT:(t + 1) * MT], ident)
                    mm.then_inc(tr_mm, 1)
                    for t in range(MB):
                        nc.tensor.matmul(ps[0:MT, 6, t * E:(t + 1) * E], yp[:, t * MT:(t + 1) * MT], wgate[:],
                                         start=True, stop=False)
                        mm = nc.tensor.matmul(ps[0:MT, 6, t * E:(t + 1) * E], ones[:, 0:MT], gate_b, start=False,
                                              stop=True)
                    mm.then_inc(gate_mm, 1)

                    def up(e):
                        for f in range(FB):
                            pe.wait_ge(hid_done, q * E * FB + e * FB + f + 1)
                            nc.tensor.matmul(ps[:, f, 0:PW], w1s[:, e * FF + f * 128:e * FF + (f + 1) * 128], yp,
                                             start=True, stop=True).then_inc(hid_mm, 1)

                    def down(e):
                        pe.wait_ge(hid_done, q * E * FB + (e + 2) * FB)
                        pe.wait_ge(exp_added, q * E + e + 1)
                        for t in range(MB):
                            dst = ps[0:MT, 4 + e % 2, t * D:(t + 1) * D]
                            nc.tensor.matmul(dst, ones[:, 0:MT], b2row[:, e * D:(e + 1) * D], start=True, stop=False)
                            for f in range(FB):
                                mm = nc.tensor.matmul(dst, hid[e % 2][:, f * PW + t * MT:f * PW + (t + 1) * MT],
                                                      w2s[:, e, f, :], start=False, stop=(f == FB - 1))
                        mm.then_inc(exp_mm, 1)

                    up(0)
                    for e in range(E):
                        if e + 1 < E:
                            up(e + 1)
                        down(e)

        @block.scalar
        def _(act):
            def norm(inst):
                for p in range(NP):
                    act.wait_ge(ln_cen, inst * NP + p + 1)
                    nc.scalar.activation(piece(bbuf[1], p), piece(bbuf[0], p), ACT.Square).then_inc(ln_sq, 1)
                for p in range(NP):
                    act.wait_ge(ln_var, inst * NP + p + 1)
                    nc.scalar.activation(piece(hbuf[0], p), ps[:, NP + p % 3, 0:PW], ACT.Ln,
                                         bias=eps[:, 0:1]).then_inc(ln_log, 1)
                    act.wait_ge(ln_log, inst * NP + p + 1)
                    nc.scalar.activation(piece(hbuf[0], p), piece(hbuf[0], p), ACT.Exp, scale=-0.5).then_inc(ln_rstd, 1)

            act.sem_inc(b_moved, 1)
            act.sem_inc(hid_done, 4)
            act.wait_ge(const_ld, 160)
            act.wait_ge(sel_made, 1)
            with act.Fori(0, HALVES) as hf:
                nc.scalar.preload_act_table_set("natural_log_exp_and_others")
                norm(hf * LN_PER_HALF)
                with act.Fori(0, LAYERS) as layer:
                    R = hf * LAYERS + layer
                    nc.scalar.preload_act_table_set("silu_and_others")
                    for q in range(4 * NP):
                        act.wait_ge(proj_mm, R * 4 * NP + q + 1)
                        dst = piece(blk(dtx, q // NP) if q < 2 * NP else blk(z, q // NP - 2), q % NP)
                        nc.scalar.activation(dst, ps[:, q % 8, 0:PW], ACT.Copy if q < 2 * NP else ACT.Silu)\
                            .then_inc(proj_ev, 1)
                    for h in range(2):
                        act.wait_ge(conv_done, R * 2 + h + 1)
                        nc.scalar.activation(blk(xc, h), blk(xc, h), ACT.Silu).then_inc(xc_ready, 1)
                    nc.scalar.preload_act_table_set("natural_log_exp_and_others")
                    for p in range(NP):
                        act.wait_ge(bc_mm, R * NP + p + 1)
                        nc.scalar.activation(piece(part[0], p), ps[:, p, 0:PW], ACT.Copy).then_inc(hi_done, 1)
                    for p in range(NP):
                        act.wait_ge(r1_done, R * NP + p + 1)
                        nc.scalar.activation(piece(part[1], p), piece(hbuf[0], p), ACT.Copy).then_inc(mid_done, 1)
                    for q in range(2 * NP):
                        act.wait_ge(dt_mm, R * 2 * NP + q + 1)
                        nc.scalar.activation(piece(blk(dt, q // NP), q % NP), ps[:, (NP + q) % 8, 0:PW], ACT.Abs,
                                             bias=dt_b[:, q // NP:q // NP + 1]).then_inc(dt_abs, 1)
                    act.wait_ge(par_ld, R * 80 + 80)
                    nc.scalar.activation(nega[:], alog, ACT.Exp).then_inc(aexp_done, 1)
                    for h in range(2):
                        act.wait_ge(dt_abs, R * 2 * NP + (h + 1) * NP)
                        nc.scalar.activation(blk(dt, h), blk(dt, h), ACT.Exp, scale=-1.0).then_inc(dt_exp, 1)
                    for h in range(2):
                        act.wait_ge(dt_exp, R * 2 + h + 1)
                        nc.scalar.activation(blk(dt, h), blk(dt, h), ACT.Ln, bias=eps[:, 1:2]).then_inc(dt_log, 1)
                    nc.scalar.preload_act_table_set("natural_log_exp_and_others")
                    act.wait_ge(nega_ready, R + 1)
                    for h in range(2):
                        H = R * 2 + h
                        act.wait_ge(dt_ready, H + 1)
                        with act.Fori(0, GSTEP // 2) as jj:
                            for v in range(4):
                                i, j, u = H * NST + jj * 4 + v, jj * 2 + v // 2, v % 2

                                def decay(part_of):
                                    im = slice(part_of * HB // 2, (part_of + 1) * HB // 2)
                                    return nc.scalar.activation(
                                        images(abuf[u][:])[:, im, 1:SEQ], images(blk(dt, h))[:, im, 1:SEQ],
                                        ACT.Exp, scale=nega[:, ds(j + (h * NST + u * GSTEP), 1)])

                                act.wait_ge(scanned, i + 1)
                                for p in range(NP):
                                    if p == 3:
                                        act.wait_ge(scanned, i + 3)
                                        decay(0)
                                    act.wait_ge(b_spread, i * NP + p + 1)
                                    nc.scalar.activation(piece(bbuf[v], p), ps[:, 5, 0:PW], ACT.Copy)\
                                        .then_inc(b_moved, 1)
                                decay(1).then_inc(a_ready, 1)
                    norm(hf * LN_PER_HALF + 1 + layer)
                norm(hf * LN_PER_HALF + 1 + LAYERS)
                norm(hf * LN_PER_HALF + 2 + LAYERS)

                act.wait_ge(ln_out, (hf + 1) * LN_PER_HALF * NP)
                with act.Fori(0, AG) as j:
                    g = hf * AG + j
                    nc.scalar.activation(hg, xs[:, ds(j * AW, AW)], ACT.Copy).then_inc(att["hg"], 1)
                    act.wait_ge(att["qkv"], g + 1)
                    nc.scalar.activation(sqk, ps[:, 0:2, 0:AW], ACT.Square)
                    nc.scalar.activation(vsb.rearrange("p b d -> p (b d)"), ps[0:SEQ, 2, :], ACT.Copy)\
                        .then_inc(att["sq"], 1)
                    act.wait_ge(att["ssq"], g + 1)
                    nc.scalar.activation(rqk, ps[:, 3:5, 0:AW], ACT.Ln, bias=small[:, 0:1]).then_inc(att["log"], 1)
                    act.wait_ge(att["log"], g + 1)
                    nc.scalar.activation(rqk, rqk, ACT.Exp, scale=-0.5).then_inc(att["r"], 1)
                    act.wait_ge(att["sub"], g + 1)
                    nc.scalar.activation(sc, sc, ACT.Exp).then_inc(att["e"], 1)
                    act.wait_ge(att["t"], g + 1)
                    nc.scalar.activation(pT.rearrange("p h b t -> p h (b t)"), ps[0:SEQ, 3:5, 0:AW], ACT.Copy)\
                        .then_inc(att["pt"], 1)
                    act.wait_ge(att["y"], g + 1)
                    nc.scalar.activation(yT[:, ds(j * AW, AW)], ps[:, 1, 0:AW], ACT.Copy).then_inc(att["yc"], 1)

                act.wait_ge(att["yc"], (hf + 1) * AG)
                with act.Fori(0, NP) as p:
                    q = hf * NP + p
                    nc.scalar.preload_act_table_set("natural_log_exp_and_others")
                    act.wait_ge(piece_done, q + 1)
                    nc.scalar.activation(yp, yT[:, ds(p * PW, PW)], ACT.Copy).then_inc(cp_done, 1)
                    nc.scalar.activation(hp, h0[:, ds(p * PW, PW)], ACT.Copy).then_inc(cp_done, 1)
                    act.wait_ge(g_sub, q + 1)
                    nc.scalar.activation(gate, lg, ACT.Exp).then_inc(g_exp, 1)
                    nc.scalar.preload_act_table_set("gelu_apprx_tanh_and_others")
                    for e in range(E):
                        act.wait_ge(exp_mm, q * E + e + 1)
                        for f in range(FB):
                            act.wait_ge(hid_mm, q * E * FB + e * FB + f + 1)
                            nc.scalar.activation(hid[e % 2][:, f * PW:(f + 1) * PW], ps[:, f, 0:PW],
                                                 ACT.Gelu_apprx_tanh, bias=vffn[:, 4 + e * FB + f:5 + e * FB + f])\
                                .then_inc(hid_done, 1)

        @block.vector
        def _(dve):
            def norm(inst, source, dst, affine=None, g=None, b=None):
                for p in range(NP):
                    dve.wait_ge(ln_mean, inst * NP + p + 1)
                    nc.vector.tensor_tensor(piece(bbuf[0], p), piece(source, p), ps[:, p, 0:PW], ALU.subtract)\
                        .then_inc(ln_cen, 1)
                for p in range(NP):
                    dve.wait_ge(ln_rstd, inst * NP + p + 1)
                    if affine is None:
                        nc.vector.tensor_tensor(piece(dst, p), piece(bbuf[0], p), piece(hbuf[0], p), ALU.mult)\
                            .then_inc(ln_out, 1)
                    else:
                        nc.vector.tensor_tensor(piece(bbuf[0], p), piece(bbuf[0], p), piece(hbuf[0], p), ALU.mult)\
                            .then_inc(ln_nrm, 1)
                        dve.wait_ge(ln_nrm, affine * NP + p + 1)
                        nc.vector.tensor_scalar(piece(dst, p), piece(bbuf[0], p), g, b, ALU.mult, ALU.add)\
                            .then_inc(ln_out, 1)

            dve.sem_inc(tok_mm, 2)
            dve.sem_inc(tok_ev, 2)
            dve.sem_inc(g_ready, 2)
            dve.sem_inc(scanned, 4)
            dve.sem_inc(y_gated, 1)
            dve.sem_inc(exp_added, 2)
            dve.sem_inc(piece_done, 1)
            for u in range(2):
                nc.vector.memset(images(abuf[u][:])[:, :, 0:1], 0.0)
            nc.vector.memset(eps[:, 0:1], EPS)
            nc.vector.memset(eps[:, 1:2], 1.0)
            nc.vector.memset(small[:, 0:1], 1e-12).then_inc(edge_zero, 1)
            dve.wait_ge(const_ld, 160)
            nc.vector.tensor_scalar(kg8[:], vffn[:, 3:4], float(DH) ** 0.5, None, ALU.mult).then_inc(kg_done, 1)
            nc.vector.tensor_copy(sel[:], eye32[:].unsqueeze(2).broadcast_to([96, GSTEP, 128])).then_inc(sel_made, 1)
            with dve.Fori(0, HALVES) as hf:
                nc.vector.tensor_scalar(images(h0[:])[:, :, 0], vtok[:, 1:2].broadcast_to([128, HB]), posT[:, 0:1],
                                        None, ALU.mult).then_inc(cls_done, 1)
                with dve.Fori(0, TOKG // 2) as j:
                    for u in range(2):
                        dve.wait_ge(tok_mm, hf * (TOKG + 2) + j * 2 + u + 3)
                        dst = images(h0[:, ds((j * 2 + u) * TOKB * SEQ, TOKB * SEQ)])[:, :, 1:SEQ]
                        nc.vector.scalar_tensor_tensor(
                            out=dst, in0=ps[:, u, 0:TOKB * 64].rearrange("p (b t) -> p b t", b=TOKB),
                            scalar=vtok[:, 0:1], in1=posT[:, 1:SEQ].unsqueeze(1).broadcast_to([128, TOKB, 64]),
                            op0=ALU.add, op1=ALU.mult).then_inc(tok_ev, 1)
                norm(hf * LN_PER_HALF, h0, xs)

                with dve.Fori(0, LAYERS) as layer:
                    R = hf * LAYERS + layer
                    dve.wait_ge(par_ld, R * 80 + 80)
                    for h in range(2):
                        ins = nc.vector.tensor_scalar(dskip[:, h, :], ident, dvec[:, h:h + 1], None, ALU.mult)
                    ins.then_inc(dskip_ready, 1)
                    for h in range(2):
                        dve.wait_ge(proj_ev, R * 4 * NP + (h + 1) * NP)
                        nc.vector.tensor_scalar(blk(xc, h), blk(dtx, h), conv_w[:, h, TAPS - 1:TAPS],
                                                conv_b[:, h:h + 1], ALU.mult, ALU.add).then_inc(conv_step, 1)
                        for s in range(1, TAPS):
                            dve.wait_ge(conv_step, (R * 2 + h) * TAPS + s)
                            now = images(blk(xc, h))[:, :, s:SEQ]
                            nc.vector.scalar_tensor_tensor(
                                out=now, in0=images(blk(dtx, h))[:, :, 0:SEQ - s],
                                scalar=conv_w[:, h, TAPS - 1 - s:TAPS - s], in1=now, op0=ALU.mult,
                                op1=ALU.add).then_inc(conv_step, 1)
                        dve.wait_ge(conv_step, (R * 2 + h + 1) * TAPS)
                        dve.sem_inc(conv_done, 1)
                    for p in range(NP):
                        dve.wait_ge(hi_done, R * NP + p + 1)
                        nc.vector.tensor_tensor(piece(hbuf[0], p), ps[:, p, 0:PW], piece(part[0], p), ALU.subtract)\
                            .then_inc(r1_done, 1)
                    for p in range(NP):
                        dve.wait_ge(mid_done, R * NP + p + 1)
                        nc.vector.tensor_tensor(piece(part[2], p), piece(hbuf[0], p), piece(part[1], p),
                                                ALU.subtract).then_inc(lo_done, 1)
                    for q in range(2 * NP):
                        dve.wait_ge(dt_abs, R * 2 * NP + q + 1)
                        nc.vector.tensor_scalar(piece(blk(dtx, q // NP), q % NP), ps[:, (NP + q) % 8, 0:PW],
                                                dt_b[:, q // NP:q // NP + 1], 0.0, ALU.add, ALU.max)\
                            .then_inc(dt_relu, 1)
                    dve.wait_ge(aexp_done, R + 1)
                    nc.vector.tensor_scalar(nega[:], nega[:], -1.0, None, ALU.mult).then_inc(nega_ready, 1)
                    for h in range(2):
                        dve.wait_ge(dt_log, R * 2 + h + 1)
                        dve.wait_ge(dt_relu, R * 2 * NP + (h + 1) * NP)
                        nc.vector.tensor_tensor(blk(dt, h), blk(dt, h), blk(dtx, h), ALU.add).then_inc(dt_ready, 1)
                    for h in range(2):
                        H = R * 2 + h
                        with dve.Fori(0, GSTEP // 2) as jj:
                            for v in range(4):
                                i, u = H * NST + jj * 4 + v, v % 2
                                dve.wait_ge(a_ready, i + 1)
                                dve.wait_ge(b_ready, i + 1)
                                dve.wait_ge(y_added, i + 1)
                                nc.vector.tensor_tensor_scan(hbuf[u][:], abuf[u][:], bbuf[v][:], 0.0, ALU.mult,
                                                             ALU.add).then_inc(scanned, 1)
                                dve.wait_ge(scanned, i + 5)
                                for p in range(NP):
                                    dve.wait_ge(c_spread, i * NP + p + 1)
                                    nc.vector.tensor_tensor(piece(hbuf[u], p), piece(hbuf[u], p),
                                                            ps[:, 6 + (u + p) % 2, 0:PW], ALU.mult).then_inc(g_ready, 1)
                        dve.wait_ge(y_sum, H + 1)
                        zz = blk(z, h).rearrange("p (n w) -> p n w", n=NP)
                        nc.vector.tensor_tensor(zz, zz, ps[:, 0:NP, 0:PW], ALU.mult).then_inc(y_gated, 1)
                    for p in range(NP):
                        dve.wait_ge(o_mm, R * NP + p + 1)
                        nc.vector.tensor_tensor(piece(hbuf[1], p), piece(xs, p), ps[:, p, 0:PW], ALU.add)\
                            .then_inc(o_res, 1)
                    norm(hf * LN_PER_HALF + 1 + layer, hbuf[1], xs, hf * (LAYERS + 1) + layer, ln_g, ln_b)
                    dve.wait_ge(ln_out, (hf * LN_PER_HALF + 2 + layer) * NP)
                    dve.sem_inc(par_used, 1)

                nc.vector.tensor_tensor(h0[:], h0[:], xs[:], ALU.add).then_inc(h1_ready, 1)
                norm(hf * LN_PER_HALF + 1 + LAYERS, h0, xs)
                norm(hf * LN_PER_HALF + 2 + LAYERS, xs, xs, hf * (LAYERS + 1) + LAYERS, vffn[:, 0:1], vffn[:, 1:2])

                with dve.Fori(0, AG) as j:
                    g = hf * AG + j
                    dve.wait_ge(kg_done, 1)
                    dve.wait_ge(att["r"], g + 1)
                    nc.vector.scalar_tensor_tensor(out=qn, in0=ps[:, 0, 0:AW], scalar=vffn[:, 2:3], in1=rqk[:, 0, :],
                                                   op0=ALU.mult, op1=ALU.mult)
                    nc.vector.scalar_tensor_tensor(out=kn, in0=ps[:, 1, 0:AW], scalar=kg8[:, 0:1], in1=rqk[:, 1, :],
                                                   op0=ALU.mult, op1=ALU.mult).then_inc(att["n"], 1)
                    s4 = sc.rearrange("p (h b t) -> p h b t", h=HEADS, b=AB)
                    s3 = sc.rearrange("p (k t) -> p k t", t=SEQ)
                    mx, rs = small[0:SEQ, 8:16], small[0:SEQ, 16:24]
                    wide = [SEQ, HEADS * AB, SEQ]
                    dve.wait_ge(att["s"], g + 1)
                    for h in range(HEADS):
                        ins = nc.vector.tensor_tensor(
                            s4[:, h], ps[0:SEQ, 5 + h, 0:AW].rearrange("p (b t) -> p b t", b=AB),
                            msk[:].unsqueeze(1).broadcast_to([SEQ, AB, SEQ]), ALU.add)
                    ins.then_inc(att["soft"], 1)
                    dve.wait_ge(att["soft"], g * 4 + 1)
                    nc.vector.tensor_reduce(mx, s3, AX_X, ALU.max).then_inc(att["soft"], 1)
                    dve.wait_ge(att["soft"], g * 4 + 2)
                    nc.vector.tensor_tensor(s3, s3, mx.unsqueeze(2).broadcast_to(wide), ALU.subtract)\
                        .then_inc(att["sub"], 1)
                    dve.wait_ge(att["e"], g + 1)
                    nc.vector.tensor_reduce(rs, s3, AX_X, ALU.add).then_inc(att["soft"], 1)
                    dve.wait_ge(att["soft"], g * 4 + 3)
                    nc.vector.reciprocal(rs, rs).then_inc(att["soft"], 1)
                    dve.wait_ge(att["soft"], g * 4 + 4)
                    nc.vector.tensor_tensor(s3, s3, rs.unsqueeze(2).broadcast_to(wide), ALU.mult)\
                        .then_inc(att["p"], 1)
                    dve.wait_ge(att["o"], g + 1)
                    nc.vector.tensor_copy(osb, ps[:, 0, 0:AW]).then_inc(att["oc"], 1)

                g3 = gate.rearrange("p (t e) -> p t e", t=MB)
                l3 = lg.rearrange("p (t e) -> p t e", t=MB)
                gm, gs = small[0:MT, 24:28], small[0:MT, 28:32]
                with dve.Fori(0, NP) as p:
                    q = hf * NP + p
                    dve.wait_ge(out_st, q * 16 + 16)
                    dve.wait_ge(tr_mm, q + 1)
                    nc.vector.tensor_copy(acc, ps[0:MT, 7, :])
                    dve.wait_ge(gate_mm, q + 1)
                    pg = ps[0:MT, 6, 0:MB * E].rearrange("p (t e) -> p t e", t=MB)
                    nc.vector.tensor_reduce(gm, pg, AX_X, ALU.max).then_inc(g_soft, 1)
                    dve.wait_ge(g_soft, q * 4 + 1)
                    nc.vector.tensor_tensor(l3, pg, gm.unsqueeze(2).broadcast_to([MT, MB, E]), ALU.subtract)\
                        .then_inc(g_sub, 1)
                    dve.wait_ge(g_exp, q + 1)
                    nc.vector.tensor_reduce(gs, g3, AX_X, ALU.add).then_inc(g_soft, 1)
                    dve.wait_ge(g_soft, q * 4 + 2)
                    nc.vector.reciprocal(gs, gs).then_inc(g_soft, 1)
                    dve.wait_ge(g_soft, q * 4 + 3)
                    nc.vector.tensor_tensor(g3, g3, gs.unsqueeze(2).broadcast_to([MT, MB, E]), ALU.mult)\
                        .then_inc(g_soft, 1)
                    dve.wait_ge(g_soft, q * 4 + 4)
                    for e in range(E):
                        dve.wait_ge(exp_mm, q * E + e + 3)
                        for t in range(MB):
                            if e:
                                dve.wait_ge(acc_step, (q * E + e - 1) * MB + t + 1)
                            nc.vector.scalar_tensor_tensor(
                                out=acc[:, t * D:(t + 1) * D], in0=ps[0:MT, 4 + e % 2, t * D:(t + 1) * D],
                                scalar=gate[:, t * E + e:t * E + e + 1], in1=acc[:, t * D:(t + 1) * D],
                                op0=ALU.mult, op1=ALU.add).then_inc(acc_step, 1)
                        dve.wait_ge(acc_step, (q * E + e + 1) * MB)
                        dve.sem_inc(exp_added, 1)
                    dve.sem_inc(piece_done, 1)
                dve.sem_inc(tok_mm, 2)

        @block.gpsimd
        def _(pool):
            with pool.Fori(0, HALVES * LAYERS) as R:
                for h in range(2):
                    pool.wait_ge(dt_ready, R * 2 + h + 1)
                    nc.gpsimd.tensor_tensor(blk(dtx, h), blk(dt, h), blk(xc, h), ALU.mult).then_inc(dtx_ready, 1)
                for h in range(2):
                    H = R * 2 + h
                    with pool.Fori(0, GSTEP // 2) as jj:
                        for v in range(4):
                            i = H * NST + jj * 4 + v
                            pool.wait_ge(dtx_ready, H + 1)
                            pool.wait_ge(b_moved, (i + 1) * NP + 1)
                            nc.gpsimd.tensor_tensor(bbuf[v][:], bbuf[v][:], blk(dtx, h), ALU.mult).then_inc(b_ready, 1)


def kernel(**inputs):
    import concourse.bacc as bacc
    from concourse.bass_utils import run_bass_kernel_spmd as run

    a = {k: np.asarray(v) for k, v in inputs.items()}

    def chan(v, n):
        return np.swapaxes(v.reshape(v.shape[0], n, 128, *v.shape[2:]), 1, 2)

    def attn(n):
        return a["L0_attn_" + n]

    def ffn(n):
        return a["L0_ffn_" + n]

    par = np.concatenate([
        chan(attn("conv_w")[:, :, 0, :], 2).reshape(LAYERS, 128, 2 * TAPS),
        chan(attn("conv_b"), 2), chan(attn("dt_b"), 2), chan(attn("D_param"), 2),
        attn("ln_g")[:, :, None], attn("ln_b")[:, :, None],
        chan(attn("A_log"), 2).reshape(LAYERS, 128, 2 * NST)], axis=2)
    v_ffn = np.concatenate([
        ffn("ln_g")[:, None], ffn("ln_b")[:, None], np.concatenate([ffn("qn_g")] * HEADS)[:, None],
        np.concatenate([ffn("kn_g")] * HEADS)[:, None], ffn("b1").reshape(E * FB, 128).T], axis=1)
    ones = np.ones((128,), np.float32)
    r_ffn = np.concatenate([ffn("gate_b"), ffn("b2").reshape(-1), ones])[None, :]
    head = np.arange(128) // DH
    consts = np.concatenate([np.eye(128), np.full((128, 128), 1.0 / D), head[:, None] == head[None, :]],
                            axis=1).astype(np.float32)
    onehot = np.concatenate([np.eye(GSTEP)] * 3, axis=0).astype(np.float32)
    mask = np.where(np.tril(np.ones((SEQ, SEQ), bool)), 0.0, -3e38).astype(np.float32)
    arrays = {
        "x": a["x"].reshape(B // TOKB, TOKB, C, GRID, PATCH, GRID, PATCH).transpose(2, 4, 0, 6, 1, 3, 5)
        .reshape(ROWS, B // TOKB * TOKE),
        "w_tok": a["L0_tok_W"].reshape(D, C, PATCH, PATCH).transpose(1, 2, 3, 0).reshape(ROWS, PATCH * D),
        "v_tok": np.stack([a["L0_tok_b"], a["L0_tok_class_token"][0]], axis=1),
        "pos": a["L0_tok_pos_embed"].T,
        "w_in": attn("in_proj_w"), "w_x": attn("x_proj_w"), "w_dt": attn("dt_w"), "w_out": attn("out_w"),
        "par": par,
        "w_att": np.concatenate([ffn("Wq"), ffn("Wk"), ffn("Wv"), ffn("Wo")], axis=1),
        "w_gate": ffn("gate_W"), "v_ffn": v_ffn, "r_ffn": r_ffn,
        "w1": ffn("W1").transpose(1, 0, 2).reshape(D, E * FF),
        "w2": ffn("W2").reshape(E, FB, 128, D).transpose(2, 0, 1, 3).reshape(128, E * FB * D),
        "consts": consts, "onehot": onehot, "mask": mask,
    }
    nc = bacc.Bacc("TRN2", target_bir_lowering=False, num_devices=1)
    fed, args = {}, []
    for name, v in arrays.items():
        v = np.ascontiguousarray(v)
        fed["in_" + name] = v
        args.append(nc.dram_tensor("in_" + name, v.shape, mybir.dt.from_np(v.dtype), kind="ExternalInput").ap())
    result = nc.dram_tensor("out", (B * SEQ, D), F32, kind="ExternalOutput").ap()
    bass_vit_tower(nc, *args, result)
    r = run(nc, [fed], core_ids=[0])
    return r.results[0]["out"].reshape(B, SEQ, D)
```

```python
from contextlib import ExitStack

import numpy as np

import concourse.bass as bass
from concourse import mybir

ALU = mybir.AluOpType
ACT = mybir.ActivationFunctionType
AX_X = mybir.AxisListType.X
F32 = mybir.dt.float32
BF16 = mybir.dt.bfloat16
ds = bass.ds

B, C, IMG, PATCH, GRID = 64, 3, 224, 28, 8
SEQ = GRID * GRID + 1
D = 128
DI = 256
NST = 64
LAYERS = 4
TAPS = 4
E, FF = 8, 512
FB = FF // 128
HEADS, DH = 2, 64
HALVES = 2
HB = B // HALVES
T = HB * SEQ
NP = 5
PW = T // NP
IND = C * PATCH * PATCH
ROWS = 112
KT = IND // ROWS
TOKB = 4
TOKG = HB // TOKB
TOKE = TOKB * 64 * KT
AB = 4
AG = HB // AB
AW = AB * SEQ
MB = 4
MT = PW // MB
NPAR = 2 * TAPS + 2 + 2 + 2 + 2 * NST
GSTEP = NST // 2
EPS = 1e-5
LN_PER_HALF = LAYERS + 3


def bass_vit_tower(nc, x, w_tok, v_tok, pos, w_in, w_x, w_dt, w_out, par, par_ln, w_att, w_gate, v_ffn, r_ffn, w1, w2,
                   consts, onehot, mask, out):
    with ExitStack() as ctx:
        def sb(name, shape, dt=F32):
            return ctx.enter_context(nc.sbuf_tensor(name, shape, dt))

        def sem(name):
            return ctx.enter_context(nc.semaphore(name))

        ps = ctx.enter_context(nc.psum_tensor("ps", [128, 8, 512], F32))

        h0 = sb("h0", [128, T])
        xs = sb("xs", [128, T])
        arena = sb("arena", [128, 4 * 2 * T])
        xc, dt, dtx, z = (arena[:, k * 2 * T:(k + 1) * 2 * T] for k in range(4))
        patch = [arena[0:ROWS, u * TOKE:(u + 1) * TOKE] for u in range(2)]
        abuf = [sb(f"decay{u}", [128, T]) for u in range(2)]
        bbuf = [sb(f"drive{v}", [128, T]) for v in range(4)]
        hbuf = [sb(f"state{v}", [128, T]) for v in range(4)]
        part = [bbuf[1 + k][:].bitcast(BF16)[:, 0:T] for k in range(3)]
        stack = sb("stack", [ROWS, 4, T], BF16)
        wtok = stack[:].rearrange("p g t -> p (g t)").bitcast(F32)[:, 0:KT * D]
        sel = sb("sel", [96, GSTEP, 128], BF16)
        eye32 = sb("eye32", [96, GSTEP])
        lw = sb("lw", [128, 2 * DI + 2 * D + 2 * DI + 2 * D])
        pk = sb("pk", [128, NPAR])
        lnp = sb("lnp", [128, 2])
        nega = sb("nega", [128, 2 * NST])
        dskip = sb("dskip", [128, 2, 128])
        cst = sb("cst", [128, 3 * 128])
        msk = sb("msk", [SEQ, SEQ])
        vtok = sb("vtok", [128, 2])
        posT = sb("posT", [128, SEQ])
        watt = sb("watt", [128, 4 * D])
        wgate = sb("wgate", [128, E])
        vffn = sb("vffn", [128, 4 + E * FB])
        rffn = sb("rffn", [1, E + E * D + 128])
        eps = sb("eps", [128, 2])
        kg8 = sb("kg8", [128, 1])
        small = sb("small", [128, 64])

        ident, mean_w, head_w = (cst[:, k * 128:(k + 1) * 128] for k in range(3))
        inw = lw[:, 0:2 * DI]
        xw = lw[:, 512:768].rearrange("p (k m) -> p k m", k=2)
        dw = lw[:, 768:1280].rearrange("p (k m) -> p k m", k=2)
        ow = lw[:, 1280:1536].rearrange("p (k m) -> p k m", k=2)
        conv_w = pk[:, 0:2 * TAPS].rearrange("p (h k) -> p h k", h=2)
        conv_b, dt_b, dvec = pk[:, 8:10], pk[:, 10:12], pk[:, 12:14]
        ln_g, ln_b = lnp[:, 0:1], lnp[:, 1:2]
        alog = pk[:, 14:14 + 2 * NST]
        gate_b, b2row, ones = rffn[:, 0:E], rffn[:, E:E + E * D], rffn[:, E + E * D:]

        const_ld = sem("const_ld")
        sel_made = sem("sel_made")
        wtok_ld = sem("wtok_ld")
        sp_step, ln_used = sem("sp_step"), sem("ln_used")
        w_ld, o_ld = sem("w_ld"), sem("o_ld")
        patch_ld = [sem("patch_ld0"), sem("patch_ld1")]
        tok_mm, tok_ev, cls_done = sem("tok_mm"), sem("tok_ev"), sem("cls_done")
        ln_mean, ln_cen, ln_sq, ln_var = sem("ln_mean"), sem("ln_cen"), sem("ln_sq"), sem("ln_var")
        ln_log, ln_rstd, ln_nrm, ln_out = sem("ln_log"), sem("ln_rstd"), sem("ln_nrm"), sem("ln_out")
        proj_mm, proj_ev = sem("proj_mm"), sem("proj_ev")
        conv_step, conv_done, xc_ready = sem("conv_step"), sem("conv_done"), sem("xc_ready")
        bc_mm, hi_done, r1_done, mid_done, lo_done = (sem(n) for n in ("bc_mm", "hi_done", "r1_done", "mid_done", "lo_done"))
        stacked = sem("stacked")
        dt_mm, dt_abs, dt_relu, dt_exp, dt_log = (sem(n) for n in ("dt_mm", "dt_abs", "dt_relu", "dt_exp", "dt_log"))
        dt_ready, dtx_ready = sem("dt_ready"), sem("dtx_ready")
        aexp_done, nega_ready, dskip_ready = sem("aexp_done"), sem("nega_ready"), sem("dskip_ready")
        edge_zero = sem("edge_zero")
        b_spread, b_moved = sem("b_spread"), sem("b_moved")
        c_spread, g_ready = sem("c_spread"), sem("g_ready")
        a_ready, b_ready = sem("a_ready"), sem("b_ready")
        scanned, y_added = sem("scanned"), sem("y_added")
        y_sum, y_gated = sem("y_sum"), sem("y_gated")
        o_mm, o_res = sem("o_mm"), sem("o_res")
        h1_ready = sem("h1_ready")
        expw_ld = sem("expw_ld")
        att = {n: sem("att_" + n) for n in ("hg", "qkv", "sq", "ssq", "log", "r", "n", "s", "soft", "sub", "e", "p",
                                            "t", "pt", "o", "oc", "y", "yc")}
        kg_done = sem("kg_done")
        cp_done, tr_mm, gate_mm = sem("cp_done"), sem("tr_mm"), sem("gate_mm")
        g_soft, g_sub, g_exp = sem("g_soft"), sem("g_sub"), sem("g_exp")
        hid_mm, hid_done = sem("hid_mm"), sem("hid_done")
        exp_mm, exp_added = sem("exp_mm"), sem("exp_added")
        acc_step = sem("acc_step")
        piece_done = sem("piece_done")
        out_st = sem("out_st")

        def piece(ap, p):
            return ap[:, p * PW:(p + 1) * PW]

        def blk(ap, h):
            return ap[:, h * T:(h + 1) * T]

        def images(ap):
            return ap.rearrange("p (b t) -> p b t", t=SEQ)

        def dt_bank(q):
            return q if q < NP else q - 3

        def bc_bank(p):
            return (NP + p) % 8

        yT = xc[:, 0:T]
        hg = bbuf[0][:, 0:AW]
        sqk = bbuf[0][:, AW:3 * AW].rearrange("p (a t) -> p a t", a=2)
        rqk = bbuf[0][:, 3 * AW:5 * AW].rearrange("p (a t) -> p a t", a=2)
        qn, kn = bbuf[0][:, 5 * AW:6 * AW], bbuf[0][:, 6 * AW:7 * AW]
        osb = bbuf[0][:, 7 * AW:8 * AW]
        vsb = bbuf[1][0:SEQ, 0:512].rearrange("p (b d) -> p b d", b=AB)
        sc = bbuf[1][0:SEQ, 512:512 + 8 * SEQ]
        pT = bbuf[1][0:SEQ, 1040:1040 + 8 * SEQ].rearrange("p (h b t) -> p h b t", h=HEADS, b=AB)
        yp, hp = hbuf[0][:, 0:PW], hbuf[0][:, PW:2 * PW]
        acc = hbuf[0][0:MT, 2 * PW:2 * PW + MB * D]
        lg = hbuf[1][0:MT, 0:MB * E]
        gate = hbuf[1][0:MT, 64:64 + MB * E]
        hid = [z[:, u * FB * PW:(u + 1) * FB * PW] for u in range(2)]
        w1s = dt[:, 0:E * FF]
        w2s = dtx[:, 0:E * FB * D].rearrange("p (e f d) -> p e f d", e=E, f=FB)

        block = ctx.enter_context(nc.Block())

        @block.sync
        def _(sp):
            for dst, src in ((vtok[:], v_tok), (posT[:], pos), (cst[:], consts),
                             (eye32[:], onehot), (msk[:], mask), (watt[:], w_att), (wgate[:], w_gate),
                             (vffn[:], v_ffn), (rffn[:], r_ffn)):
                sp.dma_start(dst, src).then_inc(const_ld, 16)
            sp.sem_inc(out_st, 16)

            def first_weights(at):
                return ((inw, w_in[at].rearrange("o p m -> (o p) m")),
                        (xw, w_x[at].rearrange("o (k p) m -> p (o k) m", p=128)),
                        (dw, w_dt[at].rearrange("o (k p) m -> p (o k) m", p=128)),
                        (pk[:], par[at].rearrange("o p m -> (o p) m")))

            def last_weights(at):
                return ((ow, w_out[at].rearrange("o (k p) m -> p (o k) m", p=128)),
                        (lnp[:], par_ln[at].rearrange("o p m -> (o p) m")))

            for dst, src in first_weights(slice(0, 1)):
                sp.dma_start(dst, src).then_inc(w_ld, 16)
            for dst, src in last_weights(slice(0, 1)):
                sp.dma_start(dst, src).then_inc(o_ld, 16)
            with sp.Fori(0, HALVES) as hf:
                sp.wait_ge(tok_mm, hf * (TOKG + 2) + 2)
                sp.dma_start(wtok, w_tok).then_inc(wtok_ld, 16)
                with sp.Fori(0, TOKG // 2) as j:
                    for u in range(2):
                        g = hf * TOKG + j * 2 + u
                        group = sp.snap(g * TOKE)
                        sp.wait_ge(tok_mm, hf * (TOKG + 2) + j * 2 + u + 1)
                        sp.dma_start(patch[u], x[:, ds(group, TOKE)]).then_inc(patch_ld[u], 16)
                with sp.Fori(0, LAYERS) as layer:
                    R = hf * LAYERS + layer
                    for k, ready in enumerate((hi_done, mid_done, lo_done)):
                        sp.wait_ge(ready, R * NP + NP)
                        for grp in range(4):
                            sp.dma_start(stack[32 * k:32 * k + 32, grp, :],
                                         part[k][32 * grp:32 * grp + 32, :]).then_inc(stacked, 16)
                    nxt = sp.snap(layer + 1)
                    sp.wait_ge(dt_relu, R * 2 * NP + 2 * NP)
                    sp.sem_inc(sp_step, 1)
                    sp.wait_ge(aexp_done, R + 1)
                    for dst, src in first_weights(ds(nxt, 1)):
                        sp.dma_start(dst, src).then_inc(w_ld, 16)
                    sp.wait_ge(ln_used, R + 1)
                    for dst, src in last_weights(ds(nxt, 1)):
                        sp.dma_start(dst, src).then_inc(o_ld, 16)
                sp.wait_ge(h1_ready, hf + 1)
                sp.dma_start(w1s, w1).then_inc(expw_ld, 16)
                sp.dma_start(w2s.rearrange("p e f d -> p (e f d)"), w2).then_inc(expw_ld, 16)
                with sp.Fori(0, NP) as p:
                    q = hf * NP + p
                    row = sp.snap(q * PW)
                    sp.wait_ge(piece_done, q + 2)
                    sp.dma_start(out[ds(row, PW)].rearrange("(t p) d -> p t d", p=MT),
                                 acc.rearrange("p (t d) -> p t d", t=MB)).then_inc(out_st, 16)
            sp.wait_ge(w_ld, 64 * (HALVES * LAYERS + 1))
            sp.wait_ge(o_ld, 32 * (HALVES * LAYERS + 1))
            sp.wait_ge(out_st, 16 * (HALVES * NP + 1))

        @block.tensor
        def _(pe):
            def norm(inst, source, src_ready, src_count):
                for p in range(NP):
                    pe.wait_ge(src_ready, src_count[p])
                    nc.tensor.matmul(ps[:, p, 0:PW], mean_w, piece(source, p), start=True, stop=True).then_inc(ln_mean, 1)
                for p in range(NP):
                    pe.wait_ge(ln_sq, inst * NP + p + 1)
                    if p >= 3:
                        pe.wait_ge(ln_log, inst * NP + p - 2)
                    nc.tensor.matmul(ps[:, NP + p % 3, 0:PW], mean_w, piece(bbuf[1], p), start=True,
                                     stop=True).then_inc(ln_var, 1)

            pe.sem_inc(y_added, 4)
            pe.sem_inc(exp_mm, 2)
            pe.wait_ge(const_ld, 144)
            pe.wait_ge(sel_made, 1)
            with pe.Fori(0, HALVES) as hf:
                with pe.Fori(0, TOKG // 2) as j:
                    for u in range(2):
                        g = hf * TOKG + j * 2 + u
                        pe.wait_ge(wtok_ld, hf * 16 + 16)
                        pe.wait_ge(patch_ld[u], (hf * (TOKG // 2) + j) * 16 + 16)
                        pe.wait_ge(tok_ev, g + 1)
                        for k in range(KT):
                            mm = nc.tensor.matmul(
                                ps[:, u, 0:TOKB * 64], wtok[:, k * D:(k + 1) * D],
                                patch[u][:, k * TOKB * 64:(k + 1) * TOKB * 64], start=(k == 0),
                                stop=(k == KT - 1))
                        mm.then_inc(tok_mm, 1)
                pe.wait_ge(cls_done, hf + 1)
                norm(hf * LN_PER_HALF, h0, tok_ev, [(hf + 1) * TOKG + 2] * NP)

                with pe.Fori(0, LAYERS) as layer:
                    R = hf * LAYERS + layer
                    pe.wait_ge(w_ld, R * 64 + 64)
                    for q in range(4 * NP):
                        if q < NP:
                            pe.wait_ge(ln_out, (hf * LN_PER_HALF + layer) * NP + q + 1)
                        if q >= 8:
                            pe.wait_ge(proj_ev, R * 4 * NP + q - 7)
                        nc.tensor.matmul(ps[:, q % 8, 0:PW], inw[:, (q // NP) * 128:(q // NP + 1) * 128],
                                         piece(xs, q % NP), start=True, stop=True).then_inc(proj_mm, 1)
                    def dt_product(q):
                        for k in range(2):
                            mm = nc.tensor.matmul(ps[:, dt_bank(q), 0:PW],
                                                  dw[:, k, (q // NP) * 128:(q // NP + 1) * 128],
                                                  piece(blk(xc, k), q % NP), start=(k == 0), stop=(k == 1))
                        mm.then_inc(dt_mm, 1)

                    pe.wait_ge(xc_ready, R * 2 + 2)
                    for q in range(NP):
                        dt_product(q)
                    for p in range(NP):
                        if p >= 3:
                            pe.wait_ge(dt_relu, R * 2 * NP + p - 2)
                        for k in range(2):
                            mm = nc.tensor.matmul(ps[:, bc_bank(p), 0:PW], xw[:, k, :], piece(blk(xc, k), p),
                                                  start=(k == 0), stop=(k == 1))
                        mm.then_inc(bc_mm, 1)
                    for q in range(NP, 2 * NP):
                        if q < NP + 3:
                            pe.wait_ge(dt_relu, R * 2 * NP + q - 2)
                        else:
                            pe.wait_ge(r1_done, R * NP + q - 7)
                        dt_product(q)
                    pe.wait_ge(dskip_ready, R + 1)
                    pe.wait_ge(dt_relu, R * 2 * NP + 2 * NP)
                    pe.wait_ge(r1_done, R * NP + NP)
                    pe.wait_ge(stacked, R * 192 + 192)
                    for h in range(2):
                        H = R * 2 + h
                        pe.wait_ge(y_gated, H + 1)

                        def spread_b(i, u, j, p):
                            pe.wait_ge(b_moved, (H * NST + i) * NP + p + 1)
                            nc.tensor.matmul(ps[:, 5, 0:PW], sel_row(j), stack[0:96, u, p * PW:(p + 1) * PW],
                                             start=True, stop=True).then_inc(b_spread, 1)

                        def spread_c(i, u, j, p):
                            pe.wait_ge(g_ready, (H * NST + i) * NP + p + 1)
                            nc.tensor.matmul(ps[:, 6 + (u + p) % 2, 0:PW], sel_row(j),
                                             stack[0:96, 2 + u, p * PW:(p + 1) * PW],
                                             start=True, stop=True).then_inc(c_spread, 1)

                        def step(jj, v, first=False, last=False):
                            u, j = v % 2, 2 * jj + v // 2
                            i = 2 * j + u

                            def b_of(p):
                                if not last or v == 0:
                                    spread_b(i + 3, 1 - u, j + 1 + u, p)
                                elif h == 0:
                                    spread_b(i + 3, (v - 1) % 2, (v - 1) // 2, p)

                            def y_of(p):
                                if not first:
                                    add_y(i - 1, (v - 1) % 4, p)

                            spread_c(i, u, j, 0)
                            spread_c(i, u, j, 1)
                            for p in range(3):
                                y_of(p)
                                b_of(p)
                            spread_c(i, u, j, 2)
                            y_of(3)
                            spread_c(i, u, j, 3)
                            b_of(3)
                            spread_c(i, u, j, 4)
                            y_of(4)
                            b_of(4)

                        def add_y(i, v, p, last=False):
                            pe.wait_ge(g_ready, (H * NST + i) * NP + p + 3)
                            mm = nc.tensor.matmul(ps[:, p, 0:PW], ident, piece(hbuf[v], p), start=False,
                                                  stop=last, skip_group_check=True)
                            if p == NP - 1:
                                mm.then_inc(y_added, 1)

                        def sel_row(j):
                            return sel[:, ds(j, 1), :].rearrange("p o m -> p (o m)")

                        for p in range(NP):
                            nc.tensor.matmul(ps[:, p, 0:PW], dskip[:, h, :], piece(blk(xc, h), p), start=True,
                                             stop=False, skip_group_check=True)
                        if h == 0:
                            for i in range(3):
                                for p in range(NP):
                                    spread_b(i, i % 2, i // 2, p)
                        for v in range(4):
                            step(0, v, first=(v == 0))
                        with pe.Fori(1, NST // 4 - 1) as jj:
                            for v in range(4):
                                step(jj, v)
                        for v in range(4):
                            step(NST // 4 - 1, v, last=True)
                        for p in range(NP):
                            add_y(NST - 1, 3, p, last=True)
                        pe.wait_ge(y_added, (H + 1) * NST + 4)
                        pe.sem_inc(y_sum, 1)
                    pe.wait_ge(o_ld, R * 32 + 32)
                    for p in range(NP):
                        pe.wait_ge(y_gated, R * 2 + 3)
                        for k in range(2):
                            mm = nc.tensor.matmul(ps[:, p, 0:PW], ow[:, k, :], piece(blk(z, k), p), start=(k == 0),
                                                  stop=(k == 1))
                        mm.then_inc(o_mm, 1)
                    norm(hf * LN_PER_HALF + 1 + layer, hbuf[1], o_res, [R * NP + p + 1 for p in range(NP)])

                norm(hf * LN_PER_HALF + 1 + LAYERS, h0, h1_ready, [hf + 1] * NP)
                norm(hf * LN_PER_HALF + 2 + LAYERS, xs, ln_out,
                     [(hf * LN_PER_HALF + LAYERS + 1) * NP + p + 1 for p in range(NP)])

                with pe.Fori(0, AG) as j:
                    g = hf * AG + j
                    pe.wait_ge(att["hg"], g + 1)
                    for k in range(2):
                        nc.tensor.matmul(ps[:, k, 0:AW], watt[:, k * D:(k + 1) * D], hg, start=True, stop=True)
                    for b in range(AB):
                        mm = nc.tensor.matmul(ps[0:SEQ, 2, b * D:(b + 1) * D], hg[:, b * SEQ:(b + 1) * SEQ],
                                              watt[:, 2 * D:3 * D], start=True, stop=True)
                    mm.then_inc(att["qkv"], 1)
                    pe.wait_ge(att["sq"], g + 1)
                    for k in range(2):
                        mm = nc.tensor.matmul(ps[:, 3 + k, 0:AW], head_w, sqk[:, k, :], start=True, stop=True)
                    mm.then_inc(att["ssq"], 1)
                    pe.wait_ge(att["n"], g + 1)
                    for h in range(HEADS):
                        hd = slice(h * DH, (h + 1) * DH)
                        for b in range(AB):
                            tk = slice(b * SEQ, (b + 1) * SEQ)
                            mm = nc.tensor.matmul(ps[0:SEQ, 5 + h, tk], qn[hd, tk], kn[hd, tk], start=True, stop=True)
                    mm.then_inc(att["s"], 1)
                    pe.wait_ge(att["p"], g + 1)
                    for h in range(HEADS):
                        for b in range(AB):
                            k = h * AB + b
                            mm = nc.tensor.transpose(ps[0:SEQ, 3 + h, b * SEQ:(b + 1) * SEQ],
                                                     sc[:, k * SEQ:(k + 1) * SEQ], ident[0:SEQ, 0:SEQ])
                    mm.then_inc(att["t"], 1)
                    pe.wait_ge(att["pt"], g + 1)
                    for h in range(HEADS):
                        hd = slice(h * DH, (h + 1) * DH)
                        for b in range(AB):
                            mm = nc.tensor.matmul(ps[hd, 0, b * SEQ:(b + 1) * SEQ], vsb[:, b, hd], pT[:, h, b, :],
                                                  start=True, stop=True)
                    mm.then_inc(att["o"], 1)
                    pe.wait_ge(att["oc"], g + 1)
                    nc.tensor.matmul(ps[:, 1, 0:AW], watt[:, 3 * D:4 * D], osb, start=True,
                                     stop=True).then_inc(att["y"], 1)

                with pe.Fori(0, NP) as p:
                    q = hf * NP + p
                    pe.wait_ge(expw_ld, hf * 32 + 32)
                    pe.wait_ge(cp_done, q * 2 + 2)
                    for t in range(MB):
                        mm = nc.tensor.transpose(ps[0:MT, 7, t * D:(t + 1) * D], hp[:, t * MT:(t + 1) * MT], ident)
                    mm.then_inc(tr_mm, 1)
                    for t in range(MB):
                        nc.tensor.matmul(ps[0:MT, 6, t * E:(t + 1) * E], yp[:, t * MT:(t + 1) * MT], wgate[:],
                                         start=True, stop=False)
                        mm = nc.tensor.matmul(ps[0:MT, 6, t * E:(t + 1) * E], ones[:, 0:MT], gate_b, start=False,
                                              stop=True)
                    mm.then_inc(gate_mm, 1)

                    def up(e):
                        for f in range(FB):
                            pe.wait_ge(hid_done, q * E * FB + e * FB + f + 1)
                            nc.tensor.matmul(ps[:, f, 0:PW], w1s[:, e * FF + f * 128:e * FF + (f + 1) * 128], yp,
                                             start=True, stop=True).then_inc(hid_mm, 1)

                    def down(e):
                        pe.wait_ge(hid_done, q * E * FB + (e + 2) * FB)
                        pe.wait_ge(exp_added, q * E + e + 1)
                        for t in range(MB):
                            dst = ps[0:MT, 4 + e % 2, t * D:(t + 1) * D]
                            nc.tensor.matmul(dst, ones[:, 0:MT], b2row[:, e * D:(e + 1) * D], start=True, stop=False)
                            for f in range(FB):
                                mm = nc.tensor.matmul(dst, hid[e % 2][:, f * PW + t * MT:f * PW + (t + 1) * MT],
                                                      w2s[:, e, f, :], start=False, stop=(f == FB - 1))
                        mm.then_inc(exp_mm, 1)

                    up(0)
                    for e in range(E):
                        if e + 1 < E:
                            up(e + 1)
                        down(e)

        @block.scalar
        def _(act):
            def norm(inst):
                for p in range(NP):
                    act.wait_ge(ln_cen, inst * NP + p + 1)
                    nc.scalar.activation(piece(bbuf[1], p), piece(bbuf[0], p), ACT.Square).then_inc(ln_sq, 1)
                for p in range(NP):
                    act.wait_ge(ln_var, inst * NP + p + 1)
                    nc.scalar.activation(piece(hbuf[0], p), ps[:, NP + p % 3, 0:PW], ACT.Ln,
                                         bias=eps[:, 0:1]).then_inc(ln_log, 1)
                    act.wait_ge(ln_log, inst * NP + p + 1)
                    nc.scalar.activation(piece(hbuf[0], p), piece(hbuf[0], p), ACT.Exp, scale=-0.5).then_inc(ln_rstd, 1)

            act.sem_inc(b_moved, 1)
            act.sem_inc(hid_done, 4)
            act.wait_ge(const_ld, 144)
            act.wait_ge(sel_made, 1)
            with act.Fori(0, HALVES) as hf:
                nc.scalar.preload_act_table_set("natural_log_exp_and_others")
                norm(hf * LN_PER_HALF)
                with act.Fori(0, LAYERS) as layer:
                    R = hf * LAYERS + layer
                    nc.scalar.preload_act_table_set("silu_and_others")
                    for q in range(4 * NP):
                        act.wait_ge(proj_mm, R * 4 * NP + q + 1)
                        dst = piece(blk(dtx, q // NP) if q < 2 * NP else blk(z, q // NP - 2), q % NP)
                        nc.scalar.activation(dst, ps[:, q % 8, 0:PW], ACT.Copy if q < 2 * NP else ACT.Silu)\
                            .then_inc(proj_ev, 1)
                    for h in range(2):
                        act.wait_ge(conv_done, R * 2 + h + 1)
                        nc.scalar.activation(blk(xc, h), blk(xc, h), ACT.Silu).then_inc(xc_ready, 1)
                    nc.scalar.preload_act_table_set("natural_log_exp_and_others")
                    def dt_log_part(h):
                        act.wait_ge(dt_abs, R * 2 * NP + (h + 1) * NP)
                        nc.scalar.activation(blk(dt, h), blk(dt, h), ACT.Exp, scale=-1.0).then_inc(dt_exp, 1)
                        act.wait_ge(dt_exp, R * 2 + h + 1)
                        nc.scalar.activation(blk(dt, h), blk(dt, h), ACT.Ln, bias=eps[:, 1:2]).then_inc(dt_log, 1)

                    def dt_abs_part(h):
                        for q in range(h * NP, (h + 1) * NP):
                            act.wait_ge(dt_mm, R * 2 * NP + q + 1)
                            nc.scalar.activation(piece(blk(dt, h), q % NP), ps[:, dt_bank(q), 0:PW], ACT.Abs,
                                                 bias=dt_b[:, h:h + 1]).then_inc(dt_abs, 1)

                    dt_abs_part(0)
                    for p in range(NP):
                        act.wait_ge(bc_mm, R * NP + p + 1)
                        nc.scalar.activation(piece(part[0], p), ps[:, bc_bank(p), 0:PW], ACT.Copy).then_inc(hi_done, 1)
                    dt_log_part(0)
                    for p in range(NP):
                        act.wait_ge(r1_done, R * NP + p + 1)
                        nc.scalar.activation(piece(part[1], p), piece(hbuf[0], p), ACT.Copy).then_inc(mid_done, 1)
                    nc.scalar.activation(nega[:], alog, ACT.Exp).then_inc(aexp_done, 1)
                    dt_abs_part(1)
                    dt_log_part(1)
                    nc.scalar.preload_act_table_set("natural_log_exp_and_others")
                    act.wait_ge(nega_ready, R + 1)
                    for h in range(2):
                        H = R * 2 + h
                        act.wait_ge(dt_ready, H + 1)

                        def decay(jj, v, part_of):
                            im = slice(part_of * HB // 4, (part_of + 1) * HB // 4)
                            column = jj * 2 + (h * NST + (v % 2) * GSTEP + v // 2)
                            return nc.scalar.activation(
                                images(abuf[v % 2][:])[:, im, 1:SEQ], images(blk(dt, h))[:, im, 1:SEQ],
                                ACT.Exp, scale=nega[:, ds(column, 1)])

                        def move_b(jj, v, first=False):
                            i = jj * 4 + v + H * NST
                            before = (jj, v - 1) if v else (jj - 1, 3)
                            act.wait_ge(scanned, i + 1)
                            for p in range(NP):
                                if p == 0 and not first:
                                    act.wait_ge(scanned, i + 2)
                                if p < 4 and not first:
                                    ins = decay(*before, p)
                                    if p == 3:
                                        ins.then_inc(a_ready, 1)
                                act.wait_ge(b_spread, i * NP + p + 1)
                                nc.scalar.activation(piece(bbuf[v], p), ps[:, 5, 0:PW], ACT.Copy).then_inc(b_moved, 1)

                        for v in range(4):
                            move_b(0, v, first=(v == 0))
                        with act.Fori(1, NST // 4) as jj:
                            for v in range(4):
                                move_b(jj, v)
                        act.wait_ge(scanned, (H + 1) * NST + 2)
                        for k in range(3):
                            decay(NST // 4 - 1, 3, k)
                        decay(NST // 4 - 1, 3, 3).then_inc(a_ready, 1)
                    norm(hf * LN_PER_HALF + 1 + layer)
                norm(hf * LN_PER_HALF + 1 + LAYERS)
                norm(hf * LN_PER_HALF + 2 + LAYERS)

                act.wait_ge(ln_out, (hf + 1) * LN_PER_HALF * NP)
                with act.Fori(0, AG) as j:
                    g = hf * AG + j
                    nc.scalar.activation(hg, xs[:, ds(j * AW, AW)], ACT.Copy).then_inc(att["hg"], 1)
                    act.wait_ge(att["qkv"], g + 1)
                    nc.scalar.activation(sqk, ps[:, 0:2, 0:AW], ACT.Square)
                    nc.scalar.activation(vsb.rearrange("p b d -> p (b d)"), ps[0:SEQ, 2, :], ACT.Copy)\
                        .then_inc(att["sq"], 1)
                    act.wait_ge(att["ssq"], g + 1)
                    nc.scalar.activation(rqk, ps[:, 3:5, 0:AW], ACT.Ln, bias=small[:, 0:1]).then_inc(att["log"], 1)
                    act.wait_ge(att["log"], g + 1)
                    nc.scalar.activation(rqk, rqk, ACT.Exp, scale=-0.5).then_inc(att["r"], 1)
                    act.wait_ge(att["sub"], g + 1)
                    nc.scalar.activation(sc, sc, ACT.Exp).then_inc(att["e"], 1)
                    act.wait_ge(att["t"], g + 1)
                    nc.scalar.activation(pT.rearrange("p h b t -> p h (b t)"), ps[0:SEQ, 3:5, 0:AW], ACT.Copy)\
                        .then_inc(att["pt"], 1)
                    act.wait_ge(att["y"], g + 1)
                    nc.scalar.activation(yT[:, ds(j * AW, AW)], ps[:, 1, 0:AW], ACT.Copy).then_inc(att["yc"], 1)

                act.wait_ge(att["yc"], (hf + 1) * AG)
                with act.Fori(0, NP) as p:
                    q = hf * NP + p
                    nc.scalar.preload_act_table_set("natural_log_exp_and_others")
                    act.wait_ge(piece_done, q + 1)
                    nc.scalar.activation(yp, yT[:, ds(p * PW, PW)], ACT.Copy).then_inc(cp_done, 1)
                    nc.scalar.activation(hp, h0[:, ds(p * PW, PW)], ACT.Copy).then_inc(cp_done, 1)
                    act.wait_ge(g_sub, q + 1)
                    nc.scalar.activation(gate, lg, ACT.Exp).then_inc(g_exp, 1)
                    nc.scalar.preload_act_table_set("gelu_apprx_tanh_and_others")
                    for e in range(E):
                        act.wait_ge(exp_mm, q * E + e + 1)
                        for f in range(FB):
                            act.wait_ge(hid_mm, q * E * FB + e * FB + f + 1)
                            nc.scalar.activation(hid[e % 2][:, f * PW:(f + 1) * PW], ps[:, f, 0:PW],
                                                 ACT.Gelu_apprx_tanh, bias=vffn[:, 4 + e * FB + f:5 + e * FB + f])\
                                .then_inc(hid_done, 1)

        @block.vector
        def _(dve):
            def norm(inst, source, dst, affine=None, g=None, b=None):
                for p in range(NP):
                    dve.wait_ge(ln_mean, inst * NP + p + 1)
                    nc.vector.tensor_tensor(piece(bbuf[0], p), piece(source, p), ps[:, p, 0:PW], ALU.subtract)\
                        .then_inc(ln_cen, 1)
                for p in range(NP):
                    dve.wait_ge(ln_rstd, inst * NP + p + 1)
                    if affine is None:
                        nc.vector.tensor_tensor(piece(dst, p), piece(bbuf[0], p), piece(hbuf[0], p), ALU.mult)\
                            .then_inc(ln_out, 1)
                    else:
                        nc.vector.tensor_tensor(piece(bbuf[0], p), piece(bbuf[0], p), piece(hbuf[0], p), ALU.mult)\
                            .then_inc(ln_nrm, 1)
                        dve.wait_ge(ln_nrm, affine * NP + p + 1)
                        nc.vector.tensor_scalar(piece(dst, p), piece(bbuf[0], p), g, b, ALU.mult, ALU.add)\
                            .then_inc(ln_out, 1)

            dve.sem_inc(tok_mm, 2)
            dve.sem_inc(tok_ev, 2)
            dve.sem_inc(g_ready, 2)
            dve.sem_inc(scanned, 4)
            dve.sem_inc(y_gated, 1)
            dve.sem_inc(exp_added, 2)
            dve.sem_inc(piece_done, 1)
            for u in range(2):
                nc.vector.memset(images(abuf[u][:])[:, :, 0:1], 0.0)
            nc.vector.memset(eps[:, 0:1], EPS)
            nc.vector.memset(eps[:, 1:2], 1.0)
            nc.vector.memset(small[:, 0:1], 1e-12).then_inc(edge_zero, 1)
            dve.wait_ge(const_ld, 144)
            nc.vector.tensor_scalar(kg8[:], vffn[:, 3:4], float(DH) ** 0.5, None, ALU.mult).then_inc(kg_done, 1)
            nc.vector.tensor_copy(sel[:], eye32[:].unsqueeze(2).broadcast_to([96, GSTEP, 128])).then_inc(sel_made, 1)
            with dve.Fori(0, HALVES) as hf:
                nc.vector.tensor_scalar(images(h0[:])[:, :, 0], vtok[:, 1:2].broadcast_to([128, HB]), posT[:, 0:1],
                                        None, ALU.mult).then_inc(cls_done, 1)
                with dve.Fori(0, TOKG // 2) as j:
                    for u in range(2):
                        dve.wait_ge(tok_mm, hf * (TOKG + 2) + j * 2 + u + 3)
                        dst = images(h0[:, ds((j * 2 + u) * TOKB * SEQ, TOKB * SEQ)])[:, :, 1:SEQ]
                        nc.vector.scalar_tensor_tensor(
                            out=dst, in0=ps[:, u, 0:TOKB * 64].rearrange("p (b t) -> p b t", b=TOKB),
                            scalar=vtok[:, 0:1], in1=posT[:, 1:SEQ].unsqueeze(1).broadcast_to([128, TOKB, 64]),
                            op0=ALU.add, op1=ALU.mult).then_inc(tok_ev, 1)
                norm(hf * LN_PER_HALF, h0, xs)

                with dve.Fori(0, LAYERS) as layer:
                    R = hf * LAYERS + layer
                    dve.wait_ge(w_ld, R * 64 + 64)
                    for h in range(2):
                        ins = nc.vector.tensor_scalar(dskip[:, h, :], ident, dvec[:, h:h + 1], None, ALU.mult)
                    ins.then_inc(dskip_ready, 1)
                    for h in range(2):
                        dve.wait_ge(proj_ev, R * 4 * NP + (h + 1) * NP)
                        nc.vector.tensor_scalar(blk(xc, h), blk(dtx, h), conv_w[:, h, TAPS - 1:TAPS],
                                                conv_b[:, h:h + 1], ALU.mult, ALU.add).then_inc(conv_step, 1)
                        for s in range(1, TAPS):
                            dve.wait_ge(conv_step, (R * 2 + h) * TAPS + s)
                            now = images(blk(xc, h))[:, :, s:SEQ]
                            nc.vector.scalar_tensor_tensor(
                                out=now, in0=images(blk(dtx, h))[:, :, 0:SEQ - s],
                                scalar=conv_w[:, h, TAPS - 1 - s:TAPS - s], in1=now, op0=ALU.mult,
                                op1=ALU.add).then_inc(conv_step, 1)
                        dve.wait_ge(conv_step, (R * 2 + h + 1) * TAPS)
                        dve.sem_inc(conv_done, 1)
                    def relu_part(h):
                        for q in range(h * NP, (h + 1) * NP):
                            dve.wait_ge(dt_abs, R * 2 * NP + q + 1)
                            nc.vector.tensor_scalar(piece(blk(dtx, h), q % NP), ps[:, dt_bank(q), 0:PW],
                                                    dt_b[:, h:h + 1], 0.0, ALU.add, ALU.max).then_inc(dt_relu, 1)

                    def dt_sum(h):
                        dve.wait_ge(dt_log, R * 2 + h + 1)
                        dve.wait_ge(dt_relu, R * 2 * NP + (h + 1) * NP)
                        nc.vector.tensor_tensor(blk(dt, h), blk(dt, h), blk(dtx, h), ALU.add).then_inc(dt_ready, 1)

                    relu_part(0)
                    for p in range(NP):
                        dve.wait_ge(hi_done, R * NP + p + 1)
                        nc.vector.tensor_tensor(piece(hbuf[0], p), ps[:, bc_bank(p), 0:PW], piece(part[0], p),
                                                ALU.subtract).then_inc(r1_done, 1)
                    dt_sum(0)
                    for p in range(NP):
                        dve.wait_ge(mid_done, R * NP + p + 1)
                        nc.vector.tensor_tensor(piece(part[2], p), piece(hbuf[0], p), piece(part[1], p),
                                                ALU.subtract).then_inc(lo_done, 1)
                    dve.wait_ge(aexp_done, R + 1)
                    nc.vector.tensor_scalar(nega[:], nega[:], -1.0, None, ALU.mult).then_inc(nega_ready, 1)
                    relu_part(1)
                    dt_sum(1)
                    for h in range(2):
                        H = R * 2 + h

                        def weigh(i, v):
                            dve.wait_ge(scanned, i + 5)
                            for p in range(NP):
                                dve.wait_ge(c_spread, i * NP + p + 1)
                                nc.vector.tensor_tensor(piece(hbuf[v], p), piece(hbuf[v], p),
                                                        ps[:, 6 + (v + p) % 2, 0:PW], ALU.mult).then_inc(g_ready, 1)

                        def step(jj, v, first=False):
                            i = jj * 4 + v + H * NST
                            dve.wait_ge(a_ready, i + 1)
                            dve.wait_ge(b_ready, i + 1)
                            dve.wait_ge(y_added, i + 1)
                            nc.vector.tensor_tensor_scan(hbuf[v][:], abuf[v % 2][:], bbuf[v][:], 0.0, ALU.mult,
                                                         ALU.add).then_inc(scanned, 1)
                            if not first:
                                weigh(i - 1, (v - 1) % 4)

                        for v in range(4):
                            step(0, v, first=(v == 0))
                        with dve.Fori(1, NST // 4) as jj:
                            for v in range(4):
                                step(jj, v)
                        weigh(H * NST + NST - 1, 3)
                        dve.wait_ge(y_sum, H + 1)
                        zz = blk(z, h).rearrange("p (n w) -> p n w", n=NP)
                        nc.vector.tensor_tensor(zz, zz, ps[:, 0:NP, 0:PW], ALU.mult).then_inc(y_gated, 1)
                    for p in range(NP):
                        dve.wait_ge(o_mm, R * NP + p + 1)
                        nc.vector.tensor_tensor(piece(hbuf[1], p), piece(xs, p), ps[:, p, 0:PW], ALU.add)\
                            .then_inc(o_res, 1)
                    dve.wait_ge(o_ld, R * 32 + 32)
                    norm(hf * LN_PER_HALF + 1 + layer, hbuf[1], xs, hf * (LAYERS + 1) + layer, ln_g, ln_b)
                    dve.wait_ge(ln_out, (hf * LN_PER_HALF + 2 + layer) * NP)
                    dve.sem_inc(ln_used, 1)

                nc.vector.tensor_tensor(h0[:], h0[:], xs[:], ALU.add).then_inc(h1_ready, 1)
                norm(hf * LN_PER_HALF + 1 + LAYERS, h0, xs)
                norm(hf * LN_PER_HALF + 2 + LAYERS, xs, xs, hf * (LAYERS + 1) + LAYERS, vffn[:, 0:1], vffn[:, 1:2])

                with dve.Fori(0, AG) as j:
                    g = hf * AG + j
                    dve.wait_ge(kg_done, 1)
                    dve.wait_ge(att["r"], g + 1)
                    nc.vector.scalar_tensor_tensor(out=qn, in0=ps[:, 0, 0:AW], scalar=vffn[:, 2:3], in1=rqk[:, 0, :],
                                                   op0=ALU.mult, op1=ALU.mult)
                    nc.vector.scalar_tensor_tensor(out=kn, in0=ps[:, 1, 0:AW], scalar=kg8[:, 0:1], in1=rqk[:, 1, :],
                                                   op0=ALU.mult, op1=ALU.mult).then_inc(att["n"], 1)
                    s4 = sc.rearrange("p (h b t) -> p h b t", h=HEADS, b=AB)
                    s3 = sc.rearrange("p (k t) -> p k t", t=SEQ)
                    mx, rs = small[0:SEQ, 8:16], small[0:SEQ, 16:24]
                    wide = [SEQ, HEADS * AB, SEQ]
                    dve.wait_ge(att["s"], g + 1)
                    for h in range(HEADS):
                        ins = nc.vector.tensor_tensor(
                            s4[:, h], ps[0:SEQ, 5 + h, 0:AW].rearrange("p (b t) -> p b t", b=AB),
                            msk[:].unsqueeze(1).broadcast_to([SEQ, AB, SEQ]), ALU.add)
                    ins.then_inc(att["soft"], 1)
                    dve.wait_ge(att["soft"], g * 4 + 1)
                    nc.vector.tensor_reduce(mx, s3, AX_X, ALU.max).then_inc(att["soft"], 1)
                    dve.wait_ge(att["soft"], g * 4 + 2)
                    nc.vector.tensor_tensor(s3, s3, mx.unsqueeze(2).broadcast_to(wide), ALU.subtract)\
                        .then_inc(att["sub"], 1)
                    dve.wait_ge(att["e"], g + 1)
                    nc.vector.tensor_reduce(rs, s3, AX_X, ALU.add).then_inc(att["soft"], 1)
                    dve.wait_ge(att["soft"], g * 4 + 3)
                    nc.vector.reciprocal(rs, rs).then_inc(att["soft"], 1)
                    dve.wait_ge(att["soft"], g * 4 + 4)
                    nc.vector.tensor_tensor(s3, s3, rs.unsqueeze(2).broadcast_to(wide), ALU.mult)\
                        .then_inc(att["p"], 1)
                    dve.wait_ge(att["o"], g + 1)
                    nc.vector.tensor_copy(osb, ps[:, 0, 0:AW]).then_inc(att["oc"], 1)

                g3 = gate.rearrange("p (t e) -> p t e", t=MB)
                l3 = lg.rearrange("p (t e) -> p t e", t=MB)
                gm, gs = small[0:MT, 24:28], small[0:MT, 28:32]
                with dve.Fori(0, NP) as p:
                    q = hf * NP + p
                    dve.wait_ge(out_st, q * 16 + 16)
                    dve.wait_ge(tr_mm, q + 1)
                    nc.vector.tensor_copy(acc, ps[0:MT, 7, :])
                    dve.wait_ge(gate_mm, q + 1)
                    pg = ps[0:MT, 6, 0:MB * E].rearrange("p (t e) -> p t e", t=MB)
                    nc.vector.tensor_reduce(gm, pg, AX_X, ALU.max).then_inc(g_soft, 1)
                    dve.wait_ge(g_soft, q * 4 + 1)
                    nc.vector.tensor_tensor(l3, pg, gm.unsqueeze(2).broadcast_to([MT, MB, E]), ALU.subtract)\
                        .then_inc(g_sub, 1)
                    dve.wait_ge(g_exp, q + 1)
                    nc.vector.tensor_reduce(gs, g3, AX_X, ALU.add).then_inc(g_soft, 1)
                    dve.wait_ge(g_soft, q * 4 + 2)
                    nc.vector.reciprocal(gs, gs).then_inc(g_soft, 1)
                    dve.wait_ge(g_soft, q * 4 + 3)
                    nc.vector.tensor_tensor(g3, g3, gs.unsqueeze(2).broadcast_to([MT, MB, E]), ALU.mult)\
                        .then_inc(g_soft, 1)
                    dve.wait_ge(g_soft, q * 4 + 4)
                    for e in range(E):
                        dve.wait_ge(exp_mm, q * E + e + 3)
                        for t in range(MB):
                            if e:
                                dve.wait_ge(acc_step, (q * E + e - 1) * MB + t + 1)
                            nc.vector.scalar_tensor_tensor(
                                out=acc[:, t * D:(t + 1) * D], in0=ps[0:MT, 4 + e % 2, t * D:(t + 1) * D],
                                scalar=gate[:, t * E + e:t * E + e + 1], in1=acc[:, t * D:(t + 1) * D],
                                op0=ALU.mult, op1=ALU.add).then_inc(acc_step, 1)
                        dve.wait_ge(acc_step, (q * E + e + 1) * MB)
                        dve.sem_inc(exp_added, 1)
                    dve.sem_inc(piece_done, 1)
                dve.sem_inc(tok_mm, 2)

        @block.gpsimd
        def _(pool):
            with pool.Fori(0, HALVES * LAYERS) as R:
                for h in range(2):
                    H = R * 2 + h
                    pool.wait_ge(dt_ready, H + 1)
                    nc.gpsimd.tensor_tensor(blk(dtx, h), blk(dt, h), blk(xc, h), ALU.mult).then_inc(dtx_ready, 1)
                    with pool.Fori(0, GSTEP // 2) as jj:
                        for v in range(4):
                            i = H * NST + jj * 4 + v
                            pool.wait_ge(dtx_ready, H + 1)
                            for a, b in ((0, 3), (3, NP)):
                                w = slice(a * PW, b * PW)
                                pool.wait_ge(b_moved, i * NP + b + 1)
                                ins = nc.gpsimd.tensor_tensor(bbuf[v][:, w], bbuf[v][:, w], blk(dtx, h)[:, w],
                                                              ALU.mult)
                            ins.then_inc(b_ready, 1)


def kernel(**inputs):
    import concourse.bacc as bacc
    from concourse.bass_utils import run_bass_kernel_spmd as run

    a = {k: np.asarray(v) for k, v in inputs.items()}

    def chan(v, n):
        return np.swapaxes(v.reshape(v.shape[0], n, 128, *v.shape[2:]), 1, 2)

    def attn(n):
        return a["L0_attn_" + n]

    def ring(v):
        return np.concatenate([v, v[:1]], axis=0)

    def ffn(n):
        return a["L0_ffn_" + n]

    par = np.concatenate([
        chan(attn("conv_w")[:, :, 0, :], 2).reshape(LAYERS, 128, 2 * TAPS),
        chan(attn("conv_b"), 2), chan(attn("dt_b"), 2), chan(attn("D_param"), 2),
        chan(attn("A_log"), 2).reshape(LAYERS, 128, 2 * NST)], axis=2)
    par_ln = np.stack([attn("ln_g"), attn("ln_b")], axis=2)
    v_ffn = np.concatenate([
        ffn("ln_g")[:, None], ffn("ln_b")[:, None], np.concatenate([ffn("qn_g")] * HEADS)[:, None],
        np.concatenate([ffn("kn_g")] * HEADS)[:, None], ffn("b1").reshape(E * FB, 128).T], axis=1)
    ones = np.ones((128,), np.float32)
    r_ffn = np.concatenate([ffn("gate_b"), ffn("b2").reshape(-1), ones])[None, :]
    head = np.arange(128) // DH
    consts = np.concatenate([np.eye(128), np.full((128, 128), 1.0 / D), head[:, None] == head[None, :]],
                            axis=1).astype(np.float32)
    onehot = np.concatenate([np.eye(GSTEP)] * 3, axis=0).astype(np.float32)
    mask = np.where(np.tril(np.ones((SEQ, SEQ), bool)), 0.0, -3e38).astype(np.float32)
    arrays = {
        "x": a["x"].reshape(B // TOKB, TOKB, C, GRID, PATCH, GRID, PATCH).transpose(2, 4, 6, 0, 1, 3, 5)
        .reshape(KT, ROWS, B // TOKB, TOKB * 64).transpose(1, 2, 0, 3).reshape(ROWS, B // TOKB * TOKE),
        "w_tok": a["L0_tok_W"].reshape(D, KT, ROWS).transpose(2, 1, 0).reshape(ROWS, KT * D),
        "v_tok": np.stack([a["L0_tok_b"], a["L0_tok_class_token"][0]], axis=1),
        "pos": a["L0_tok_pos_embed"].T,
        "w_in": ring(attn("in_proj_w")), "w_x": ring(attn("x_proj_w")), "w_dt": ring(attn("dt_w")),
        "w_out": ring(attn("out_w")), "par": ring(par), "par_ln": ring(par_ln),
        "w_att": np.concatenate([ffn("Wq"), ffn("Wk"), ffn("Wv"), ffn("Wo")], axis=1),
        "w_gate": ffn("gate_W"), "v_ffn": v_ffn, "r_ffn": r_ffn,
        "w1": ffn("W1").transpose(1, 0, 2).reshape(D, E * FF),
        "w2": ffn("W2").reshape(E, FB, 128, D).transpose(2, 0, 1, 3).reshape(128, E * FB * D),
        "consts": consts, "onehot": onehot, "mask": mask,
    }
    nc = bacc.Bacc("TRN2", target_bir_lowering=False, num_devices=1)
    fed, args = {}, []
    for name, v in arrays.items():
        v = np.ascontiguousarray(v)
        fed["in_" + name] = v
        args.append(nc.dram_tensor("in_" + name, v.shape, mybir.dt.from_np(v.dtype), kind="ExternalInput").ap())
    result = nc.dram_tensor("out", (B * SEQ, D), F32, kind="ExternalOutput").ap()
    bass_vit_tower(nc, *args, result)
    r = run(nc, [fed], core_ids=[0])
    return r.results[0]["out"].reshape(B, SEQ, D)
```

```python
from contextlib import ExitStack

import numpy as np

import concourse.bass as bass
from concourse import mybir

ALU = mybir.AluOpType
ACT = mybir.ActivationFunctionType
AX_X = mybir.AxisListType.X
F32 = mybir.dt.float32
BF16 = mybir.dt.bfloat16
ds = bass.ds

B, C, IMG, PATCH, GRID = 64, 3, 224, 28, 8
SEQ = GRID * GRID + 1
D = 128
DI = 256
NST = 64
LAYERS = 4
TAPS = 4
E, FF = 8, 512
FB = FF // 128
HEADS, DH = 2, 64
HALVES = 2
HB = B // HALVES
T = HB * SEQ
NP = 5
PW = T // NP
IND = C * PATCH * PATCH
ROWS = 112
KT = IND // ROWS
TOKB = 4
TOKG = HB // TOKB
TOKE = TOKB * 64 * KT
THIRDS = 3
TK = KT // THIRDS
AB = 4
AG = HB // AB
AW = AB * SEQ
CHUNKS = 2
CI = HB // CHUNKS
CT = CI * SEQ
CUT = [(0, PW), (PW, 2 * PW), (2 * PW, CT)]
NC = len(CUT)
MB = 4
MT = PW // MB
NPAR = 2 * TAPS + 2 + 2 + 2 + 2 * NST
GSTEP = NST // 2
EPS = 1e-5
LN_PER_HALF = LAYERS + 3


def bass_vit_tower(nc, x, w_tok, v_tok, pos, w_in, w_x, w_dt, w_out, par, par_ln, w_att, w_gate, v_ffn, r_ffn, w_b2,
                   w1, w2, consts, onehot, mask, out):
    with ExitStack() as ctx:
        def sb(name, shape, dt=F32):
            return ctx.enter_context(nc.sbuf_tensor(name, shape, dt))

        def sem(name):
            return ctx.enter_context(nc.semaphore(name))

        ps = ctx.enter_context(nc.psum_tensor("ps", [128, 8, 512], F32))

        h0 = sb("h0", [128, T])
        xs = sb("xs", [128, T])
        arena = sb("arena", [128, 4 * 2 * T])
        xc, dt, dtx, z = (arena[:, k * 2 * T:(k + 1) * 2 * T] for k in range(4))
        patch = [arena[0:ROWS, u * TOKE:(u + 1) * TOKE] for u in range(2)]
        abuf = [sb(f"decay{u}", [128, T]) for u in range(2)]
        bbuf = [sb(f"drive{u}", [128, T]) for u in range(2)]
        bsp = [sb(f"b_rows{v}", [128, CT]) for v in range(4)]
        hbuf = [sb(f"state{v}", [128, T]) for v in range(4)]
        part = [bbuf[1 - k // 2][:].bitcast(BF16)[:, k % 2 * T:(k % 2 + 1) * T] for k in range(3)]
        stack = sb("stack", [ROWS, 4, T], BF16)
        wtok = stack[:].rearrange("p g t -> p (g t)").bitcast(F32)[:, 0:KT * D]
        sel = sb("sel", [96, GSTEP, 128], BF16)
        eye32 = sb("eye32", [96, GSTEP])
        lw = sb("lw", [128, 2 * DI + 2 * D + 2 * DI + 2 * D])
        pk = sb("pk", [128, NPAR])
        lnp = sb("lnp", [128, 2])
        nega = sb("nega", [128, 2 * NST])
        dskip = sb("dskip", [128, 2, 128])
        cst = sb("cst", [128, 3 * 128])
        msk = sb("msk", [SEQ, SEQ])
        vtok = sb("vtok", [128, 2])
        posT = sb("posT", [128, SEQ])
        watt = sb("watt", [128, 4 * D])
        wgate = sb("wgate", [128, E])
        vffn = sb("vffn", [128, 4 + E * FB])
        rffn = sb("rffn", [1, E + 128])
        b2 = sb("b2", [E, D])
        eps = sb("eps", [128, 2])
        kg8 = sb("kg8", [128, 1])
        small = sb("small", [128, 64])

        ident, mean_w, head_w = (cst[:, k * 128:(k + 1) * 128] for k in range(3))
        inw = lw[:, 0:2 * DI]
        xw = lw[:, 512:768].rearrange("p (k m) -> p k m", k=2)
        dw = lw[:, 768:1280].rearrange("p (k m) -> p k m", k=2)
        ow = lw[:, 1280:1536].rearrange("p (k m) -> p k m", k=2)
        conv_w = pk[:, 0:2 * TAPS].rearrange("p (h k) -> p h k", h=2)
        conv_b, dt_b, dvec = pk[:, 8:10], pk[:, 10:12], pk[:, 12:14]
        ln_g, ln_b = lnp[:, 0:1], lnp[:, 1:2]
        alog = pk[:, 14:14 + 2 * NST]
        gate_b, ones = rffn[:, 0:E], rffn[:, E:]

        const_ld = sem("const_ld")
        sel_made = sem("sel_made")
        wtok_ld = sem("wtok_ld")
        sp_step, ln_used = sem("sp_step"), sem("ln_used")
        w_ld, o_ld = sem("w_ld"), sem("o_ld")
        patch_ld = [[sem(f"patch_ld{u}_{k}") for k in range(THIRDS)] for u in range(2)]
        tok_mm, tok_ev, cls_done = sem("tok_mm"), sem("tok_ev"), sem("cls_done")
        ln_mean, ln_cen, ln_sq, ln_var = sem("ln_mean"), sem("ln_cen"), sem("ln_sq"), sem("ln_var")
        ln_log, ln_rstd, ln_nrm, ln_out = sem("ln_log"), sem("ln_rstd"), sem("ln_nrm"), sem("ln_out")
        proj_mm, proj_ev = sem("proj_mm"), sem("proj_ev")
        conv_step, conv_done, xc_ready = sem("conv_step"), sem("conv_done"), sem("xc_ready")
        bc_mm, hi_done, r1_done, mid_done, lo_done = (sem(n) for n in ("bc_mm", "hi_done", "r1_done", "mid_done", "lo_done"))
        stacked = sem("stacked")
        dt_mm, dt_abs, dt_relu, dt_exp, dt_log = (sem(n) for n in ("dt_mm", "dt_abs", "dt_relu", "dt_exp", "dt_log"))
        dt_ready, dtx_ready = sem("dt_ready"), sem("dtx_ready")
        aexp_done, nega_ready, dskip_ready = sem("aexp_done"), sem("nega_ready"), sem("dskip_ready")
        b_spread, b_moved = sem("b_spread"), sem("b_moved")
        c_spread, g_ready = sem("c_spread"), sem("g_ready")
        a_ready, b_ready = sem("a_ready"), sem("b_ready")
        scanned, y_added = sem("scanned"), sem("y_added")
        y_sum, y_gated = sem("y_sum"), sem("y_gated")
        o_mm, o_res = sem("o_mm"), sem("o_res")
        h1_ready = sem("h1_ready")
        expw_ld = sem("expw_ld")
        att = {n: sem("att_" + n) for n in ("hg", "qkv", "sq", "ssq", "log", "r", "n", "s", "soft", "sub", "e", "p",
                                            "t", "pt", "o", "oc", "y", "yc")}
        kg_done = sem("kg_done")
        gt_mm, gt_done = sem("gt_mm"), sem("gt_done")
        cp_done, tr_mm, gate_mm = sem("cp_done"), sem("tr_mm"), sem("gate_mm")
        g_soft, g_sub, g_exp = sem("g_soft"), sem("g_sub"), sem("g_exp")
        hid_mm, hid_done = sem("hid_mm"), sem("hid_done")
        exp_mm, exp_added = sem("exp_mm"), sem("exp_added")
        acc_step = sem("acc_step")
        piece_done = sem("piece_done")
        out_st = sem("out_st")

        def piece(ap, p):
            return ap[:, p * PW:(p + 1) * PW]

        def blk(ap, h):
            return ap[:, h * T:(h + 1) * T]

        def both(ap):
            return ap.rearrange("p (h t) -> p h t", h=2)

        def images(ap):
            return ap.rearrange("p (b t) -> p b t", t=SEQ)

        TURNS = ["bc0", "bc1", "dt0", "dt1", "dt2", "dt3", "bc2", "bc3", "bc4"] + [f"dt{m}" for m in range(4, 10)]
        DT_ORDER = [(0, 0), (0, 1), (1, 0), (1, 1), (0, 2), (1, 2), (0, 3), (1, 3), (0, 4), (1, 4)]

        TURN_BANK = [0, 1, 2, 3, 4, 7, 6, 5]

        def dt_bank(m):
            return TURN_BANK[TURNS.index(f"dt{m}") % 8]

        def bc_bank(p):
            return TURN_BANK[TURNS.index(f"bc{p}") % 8]

        def chunk(ap, c):
            return both(ap)[:, :, c * CT:(c + 1) * CT]

        yT = xc[:, 0:T]
        class Group:
            def __init__(self, u):
                wide, tall = (bbuf[0], bbuf[1]) if u == 0 else (hbuf[2], hbuf[3])
                self.bank = 4 * u
                self.x = wide[:, 0:AW]
                self.sqk = wide[:, AW:3 * AW].rearrange("p (a t) -> p a t", a=2)
                self.rqk = wide[:, 3 * AW:5 * AW].rearrange("p (a t) -> p a t", a=2)
                self.qn, self.kn = wide[:, 5 * AW:6 * AW], wide[:, 6 * AW:7 * AW]
                self.o = wide[:, 7 * AW:8 * AW]
                self.v = tall[0:SEQ, 0:512].rearrange("p (b d) -> p b d", b=AB)
                self.sc = tall[0:SEQ, 512:512 + 8 * SEQ]
                self.pT = tall[0:SEQ, 1040:1040 + 8 * SEQ].rearrange("p (h b t) -> p h b t", h=HEADS, b=AB)
                self.mx, self.rs = (small[0:SEQ, 8 * k:8 * k + 8] for k in (2 * u + 1, 2 * u + 2))

        pair = [Group(0), Group(1)]
        yp, hp = hbuf[0][:, 0:PW], hbuf[0][:, PW:2 * PW]
        acc = hbuf[0][0:MT, 2 * PW:2 * PW + MB * D]
        lg = hbuf[1][0:MT, 0:MB * E]
        gate = hbuf[1][0:MT, 64:64 + MB * E]
        gate_t = hbuf[1][0:E, 128:128 + PW]
        hid = [z[:, u * FB * PW:(u + 1) * FB * PW] for u in range(2)]
        w1s = dt[:, 0:E * FF]
        w2s = dtx[:, 0:E * FB * D].rearrange("p (e f d) -> p e f d", e=E, f=FB)

        block = ctx.enter_context(nc.Block())

        @block.sync
        def _(sp):
            sp.dma_start(wtok, w_tok).then_inc(wtok_ld, 16)
            for dst, src in ((vtok[:], v_tok), (posT[:], pos), (cst[:], consts),
                             (eye32[:], onehot), (msk[:], mask), (watt[:], w_att), (wgate[:], w_gate),
                             (vffn[:], v_ffn), (rffn[:], r_ffn), (b2[:], w_b2)):
                sp.dma_start(dst, src).then_inc(const_ld, 16)
            sp.sem_inc(out_st, 16)

            def first_weights(at):
                return ((inw, w_in[at].rearrange("o p m -> (o p) m")),
                        (xw, w_x[at].rearrange("o (k p) m -> p (o k) m", p=128)),
                        (dw, w_dt[at].rearrange("o (k p) m -> p (o k) m", p=128)),
                        (pk[:], par[at].rearrange("o p m -> (o p) m")))

            def last_weights(at):
                return ((ow, w_out[at].rearrange("o (k p) m -> p (o k) m", p=128)),
                        (lnp[:], par_ln[at].rearrange("o p m -> (o p) m")))

            for dst, src in first_weights(slice(0, 1)):
                sp.dma_start(dst, src).then_inc(w_ld, 16)
            for dst, src in last_weights(slice(0, 1)):
                sp.dma_start(dst, src).then_inc(o_ld, 16)
            with sp.Fori(0, HALVES) as hf:
                with sp.Fori(0, TOKG // 2) as j:
                    for u in range(2):
                        g = hf * TOKG + j * 2 + u
                        group = sp.snap(g * TOKE)
                        sp.wait_ge(tok_mm, hf * (TOKG + 2) + j * 2 + u + 1)
                        for k in range(THIRDS):
                            w = TOKE // THIRDS
                            sp.dma_start(patch[u][:, k * w:(k + 1) * w], x[:, ds(group + k * w, w)])\
                                .then_inc(patch_ld[u][k], 16)
                with sp.Fori(0, LAYERS) as layer:
                    R = hf * LAYERS + layer
                    for k, ready in enumerate((hi_done, mid_done, lo_done)):
                        sp.wait_ge(ready, R * NP + NP)
                        for grp in range(4):
                            sp.dma_start(stack[32 * k:32 * k + 32, grp, :],
                                         part[k][32 * grp:32 * grp + 32, :]).then_inc(stacked, 16)
                    nxt = sp.snap(layer + 1)
                    sp.wait_ge(dt_relu, R * 2 * NP + 2 * NP)
                    sp.sem_inc(sp_step, 1)
                    sp.wait_ge(aexp_done, R + 1)
                    for dst, src in first_weights(ds(nxt, 1)):
                        sp.dma_start(dst, src).then_inc(w_ld, 16)
                    sp.wait_ge(ln_used, R + 1)
                    for dst, src in last_weights(ds(nxt, 1)):
                        sp.dma_start(dst, src).then_inc(o_ld, 16)
                sp.wait_ge(h1_ready, hf + 1)
                sp.dma_start(w1s, w1).then_inc(expw_ld, 16)
                sp.dma_start(w2s.rearrange("p e f d -> p (e f d)"), w2).then_inc(expw_ld, 16)
                sp.dma_start(wtok, w_tok).then_inc(wtok_ld, 16)
                with sp.Fori(0, NP) as p:
                    q = hf * NP + p
                    row = sp.snap(q * PW)
                    sp.wait_ge(piece_done, q + 2)
                    sp.dma_start(out[ds(row, PW)].rearrange("(t p) d -> p t d", p=MT),
                                 acc.rearrange("p (t d) -> p t d", t=MB)).then_inc(out_st, 16)
            sp.wait_ge(wtok_ld, 16 * (HALVES + 1))
            sp.wait_ge(w_ld, 64 * (HALVES * LAYERS + 1))
            sp.wait_ge(o_ld, 32 * (HALVES * LAYERS + 1))
            sp.wait_ge(out_st, 16 * (HALVES * NP + 1))

        @block.tensor
        def _(pe):
            def norm(inst, source, src_ready, src_count):
                for p in range(NP):
                    pe.wait_ge(src_ready, src_count[p])
                    nc.tensor.matmul(ps[:, 2 + p, 0:PW], mean_w, piece(source, p), start=True, stop=True)\
                        .then_inc(ln_mean, 1)
                for p in range(NP):
                    pe.wait_ge(ln_sq, inst * NP + p + 1)
                    if p >= 3:
                        pe.wait_ge(ln_log, inst * NP + p - 2)
                    nc.tensor.matmul(ps[:, (7 + p % 3) % 8, 0:PW], mean_w, piece(bbuf[1], p), start=True,
                                     stop=True).then_inc(ln_var, 1)

            pe.sem_inc(y_added, 4)
            pe.sem_inc(exp_mm, 2)
            pe.wait_ge(const_ld, 160)
            pe.wait_ge(sel_made, 1)
            with pe.Fori(0, HALVES) as hf:
                with pe.Fori(0, TOKG // 2) as j:
                    for u in range(2):
                        g = hf * TOKG + j * 2 + u
                        pe.wait_ge(wtok_ld, hf * 16 + 16)
                        pe.wait_ge(tok_ev, g + 1)
                        for k in range(KT):
                            if k % TK == 0:
                                pe.wait_ge(patch_ld[u][k // TK], (hf * (TOKG // 2) + j) * 16 + 16)
                            mm = nc.tensor.matmul(
                                ps[:, u, 0:TOKB * 64], wtok[:, k * D:(k + 1) * D],
                                patch[u][:, k * TOKB * 64:(k + 1) * TOKB * 64], start=(k == 0),
                                stop=(k == KT - 1))
                        mm.then_inc(tok_mm, 1)
                pe.wait_ge(cls_done, hf + 1)
                norm(hf * LN_PER_HALF, h0, tok_ev, [(hf + 1) * TOKG + 2] * NP)

                with pe.Fori(0, LAYERS) as layer:
                    R = hf * LAYERS + layer
                    pe.wait_ge(w_ld, R * 64 + 64)
                    for q in range(4 * NP):
                        if q < NP:
                            pe.wait_ge(ln_out, (hf * LN_PER_HALF + layer) * NP + q + 1)
                        if q >= 8:
                            pe.wait_ge(proj_ev, R * 4 * NP + q - 7)
                        nc.tensor.matmul(ps[:, (q + 2) % 8, 0:PW], inw[:, (q // NP) * 128:(q // NP + 1) * 128],
                                         piece(xs, q % NP), start=True, stop=True).then_inc(proj_mm, 1)

                    def dt_product(m):
                        h, p = DT_ORDER[m]
                        for k in range(2):
                            mm = nc.tensor.matmul(ps[:, dt_bank(m), 0:PW], dw[:, k, h * 128:(h + 1) * 128],
                                                  piece(blk(xc, k), p), start=(k == 0), stop=(k == 1))
                        mm.then_inc(dt_mm, 1)

                    def bc_product(p):
                        for k in range(2):
                            mm = nc.tensor.matmul(ps[:, bc_bank(p), 0:PW], xw[:, k, :], piece(blk(xc, k), p),
                                                  start=(k == 0), stop=(k == 1))
                        mm.then_inc(bc_mm, 1)

                    pe.wait_ge(xc_ready, R * 4 + 2)
                    for p in range(2):
                        bc_product(p)
                    for m in range(4):
                        dt_product(m)
                    pe.wait_ge(xc_ready, R * 4 + 4)
                    for p in range(2, NP):
                        if p == 4:
                            pe.wait_ge(r1_done, R * NP + 1)
                        bc_product(p)
                    for m in range(4, 2 * NP):
                        if m == 4:
                            pe.wait_ge(r1_done, R * NP + 2)
                        elif m < 9:
                            pe.wait_ge(dt_relu, R * 2 * NP + m - 4)
                        else:
                            pe.wait_ge(r1_done, R * NP + 3)
                        dt_product(m)
                    pe.wait_ge(r1_done, R * NP + NP)
                    pe.wait_ge(stacked, R * 192 + 192)
                    for c in range(CHUNKS):
                        K = R * CHUNKS + c

                        def sel_row(j):
                            return sel[:, ds(j, 1), :].rearrange("p o m -> p (o m)")

                        def rows(group, chunk, p):
                            lo, hi = CUT[p]
                            return stack[0:96, group, chunk * CT + lo:chunk * CT + hi]

                        def width(p):
                            return slice(0, CUT[p][1] - CUT[p][0])

                        def spread_b(i, u, j, p, chunk=c):
                            pe.wait_ge(b_moved, (K * NST + i) * NC + p + 1)
                            nc.tensor.matmul(ps[:, 5, width(p)], sel_row(j), rows(u, chunk, p),
                                             start=True, stop=True).then_inc(b_spread, 1)

                        def spread_c(i, u, j, p):
                            pe.wait_ge(g_ready, (K * NST + i) * NC + p + 1)
                            nc.tensor.matmul(ps[:, 6 + (u + p) % 2, width(p)], sel_row(j), rows(2 + u, c, p),
                                             start=True, stop=True).then_inc(c_spread, 1)

                        def add_y(i, v, p, last=False):
                            lo, hi = CUT[p // 2]
                            pe.wait_ge(g_ready, (K * NST + i) * NC + p // 2 + 3)
                            if p < 4:
                                g, dst = both(hbuf[v][:])[:, p % 2, lo:hi], ps[:, p, 0:PW]
                            else:
                                g, dst = both(hbuf[v][:])[:, :, lo:hi], both(ps[:, p, 0:PW])
                            mm = nc.tensor.matmul(dst, ident, g, start=False, stop=last, skip_group_check=True)
                            if p == 4:
                                mm.then_inc(y_added, 1)
                            return mm

                        def step(jj, v, last=False, start=False):
                            u, j = v % 2, 2 * jj + v // 2
                            i = 2 * j + u

                            def b_of(p):
                                if not last or v == 0:
                                    spread_b(i + 3, 1 - u, j + 1 + u, p)
                                elif c + 1 < CHUNKS:
                                    spread_b(i + 3, (v - 1) % 2, (v - 1) // 2, p, chunk=c + 1)

                            def y_of(p):
                                add_y(i - 1, (v - 1) % 4, p)

                            spread_c(i, u, j, 0)
                            spread_c(i, u, j, 1)
                            c_turn = 1 if last and v == 3 else 2 if start else 4
                            for p in range(5):
                                if p == c_turn:
                                    spread_c(i, u, j, 2)
                                y_of(p)
                                if p < NC:
                                    b_of(p)

                        def first_rows():
                            for p in range(2):
                                spread_c(0, 0, 0, p)
                            for p in range(NC):
                                spread_b(3, 1, 1, p)

                        if c:
                            first_rows()
                        else:
                            for p in range(NC):
                                spread_b(0, 0, 0, p)
                            pe.wait_ge(dskip_ready, R + 1)
                            pe.wait_ge(dt_relu, R * 2 * NP + 2 * NP)
                        pe.wait_ge(y_gated, K + 1)
                        for k, (lo, hi) in enumerate(CUT):
                            for h in range(2):
                                if c == 0:
                                    n = 2 * k + h + NC
                                    spread_b(n // NC, n // NC % 2, n // NC // 2, n % NC)
                                dst = ps[:, 2 * k + h, 0:PW] if k < 2 else ps[:, 4, h * (hi - lo):(h + 1) * (hi - lo)]
                                nc.tensor.matmul(dst, dskip[:, h, :], blk(xc, h)[:, c * CT + lo:c * CT + hi],
                                                 start=(k < 2 or h == 0), stop=False, skip_group_check=True)
                        if c == 0:
                            first_rows()
                        spread_c(0, 0, 0, 2)
                        for v in range(1, 4):
                            step(0, v, start=True)
                        with pe.Fori(1, NST // 4 - 1) as jj:
                            for v in range(4):
                                step(jj, v)
                        for v in range(4):
                            step(NST // 4 - 1, v, last=True)
                        for p in range(5):
                            mm = add_y(NST - 1, 3, p, last=True)
                            if p in (1, 3):
                                mm.then_inc(y_sum, 1)
                    pe.wait_ge(o_ld, R * 32 + 32)
                    for p in range(NP):
                        if p == 2:
                            pe.wait_ge(y_gated, R * 2 + 3)
                        for k in range(2):
                            mm = nc.tensor.matmul(ps[:, (5 + p) % 8, 0:PW], ow[:, k, :], piece(blk(z, k), p),
                                                  start=(k == 0), stop=(k == 1))
                        mm.then_inc(o_mm, 1)
                    norm(hf * LN_PER_HALF + 1 + layer, hbuf[1], o_res, [R * NP + p + 1 for p in range(NP)])

                norm(hf * LN_PER_HALF + 1 + LAYERS, h0, h1_ready, [hf + 1] * NP)
                norm(hf * LN_PER_HALF + 2 + LAYERS, xs, ln_out,
                     [(hf * LN_PER_HALF + LAYERS + 1) * NP + p + 1 for p in range(NP)])

                with pe.Fori(0, AG // 2) as j:
                    def group(u):
                        return hf * AG + j * 2 + u

                    for u, w in enumerate(pair):
                        pe.wait_ge(att["hg"], group(u) + 1)
                        for k in range(2):
                            nc.tensor.matmul(ps[:, w.bank + k, 0:AW], watt[:, k * D:(k + 1) * D], w.x, start=True,
                                             stop=True)
                        for b in range(AB):
                            mm = nc.tensor.matmul(ps[0:SEQ, w.bank + 2, b * D:(b + 1) * D],
                                                  w.x[:, b * SEQ:(b + 1) * SEQ], watt[:, 2 * D:3 * D], start=True,
                                                  stop=True)
                        mm.then_inc(att["qkv"], 1)
                    for u, w in enumerate(pair):
                        pe.wait_ge(att["sq"], group(u) + 1)
                        for k in range(2):
                            mm = nc.tensor.matmul(ps[:, w.bank + 2 + k, 0:AW], head_w, w.sqk[:, k, :], start=True,
                                                  stop=True)
                        mm.then_inc(att["ssq"], 1)
                    for u, w in enumerate(pair):
                        pe.wait_ge(att["n"], group(u) + 1)
                        for h in range(HEADS):
                            hd = slice(h * DH, (h + 1) * DH)
                            for b in range(AB):
                                tk = slice(b * SEQ, (b + 1) * SEQ)
                                mm = nc.tensor.matmul(ps[0:SEQ, w.bank + h, tk], w.qn[hd, tk], w.kn[hd, tk],
                                                      start=True, stop=True)
                        mm.then_inc(att["s"], 1)
                    for u, w in enumerate(pair):
                        pe.wait_ge(att["p"], group(u) + 1)
                        for h in range(HEADS):
                            for b in range(AB):
                                k = h * AB + b
                                mm = nc.tensor.transpose(ps[0:SEQ, w.bank + 2 + h, b * SEQ:(b + 1) * SEQ],
                                                         w.sc[:, k * SEQ:(k + 1) * SEQ], ident[0:SEQ, 0:SEQ])
                        mm.then_inc(att["t"], 1)
                    for u, w in enumerate(pair):
                        pe.wait_ge(att["pt"], group(u) + 1)
                        for h in range(HEADS):
                            hd = slice(h * DH, (h + 1) * DH)
                            for b in range(AB):
                                mm = nc.tensor.matmul(ps[hd, w.bank, b * SEQ:(b + 1) * SEQ], w.v[:, b, hd],
                                                      w.pT[:, h, b, :], start=True, stop=True)
                        mm.then_inc(att["o"], 1)
                    for u, w in enumerate(pair):
                        pe.wait_ge(att["oc"], group(u) + 1)
                        nc.tensor.matmul(ps[:, w.bank + 1, 0:AW], watt[:, 3 * D:4 * D], w.o, start=True,
                                         stop=True).then_inc(att["y"], 1)

                with pe.Fori(0, NP) as p:
                    q = hf * NP + p
                    pe.wait_ge(expw_ld, hf * 32 + 32)
                    pe.wait_ge(cp_done, q * 2 + 2)
                    for t in range(MB):
                        nc.tensor.matmul(ps[0:MT, 6, t * E:(t + 1) * E], yp[:, t * MT:(t + 1) * MT], wgate[:],
                                         start=True, stop=False)
                        mm = nc.tensor.matmul(ps[0:MT, 6, t * E:(t + 1) * E], ones[:, 0:MT], gate_b, start=False,
                                              stop=True)
                    mm.then_inc(gate_mm, 1)
                    for t in range(MB):
                        nc.tensor.matmul(ps[0:MT, 7, t * D:(t + 1) * D], hp[:, t * MT:(t + 1) * MT], ident,
                                         start=(t == 0), stop=False, skip_group_check=True)

                    def biases():
                        pe.wait_ge(g_soft, q * 4 + 4)
                        for t in range(MB):
                            mm = nc.tensor.transpose(ps[0:E, 6, t * MT:(t + 1) * MT], gate[:, t * E:(t + 1) * E],
                                                     ident[0:MT, 0:MT])
                        mm.then_inc(gt_mm, 1)
                        pe.wait_ge(gt_done, q + 1)
                        for t in range(MB):
                            mm = nc.tensor.matmul(ps[0:MT, 7, t * D:(t + 1) * D], gate_t[:, t * MT:(t + 1) * MT],
                                                  b2[:], start=False, stop=True, skip_group_check=True)
                        mm.then_inc(tr_mm, 1)

                    def up(e):
                        for f in range(FB):
                            pe.wait_ge(hid_done, q * E * FB + e * FB + f + 1)
                            nc.tensor.matmul(ps[:, f, 0:PW], w1s[:, e * FF + f * 128:e * FF + (f + 1) * 128], yp,
                                             start=True, stop=True).then_inc(hid_mm, 1)

                    def down(e):
                        pe.wait_ge(hid_done, q * E * FB + (e + 2) * FB)
                        pe.wait_ge(exp_added, q * E + e + 1)
                        for t in range(MB):
                            dst = ps[0:MT, 4 + e % 2, t * D:(t + 1) * D]
                            for f in range(FB):
                                mm = nc.tensor.matmul(dst, hid[e % 2][:, f * PW + t * MT:f * PW + (t + 1) * MT],
                                                      w2s[:, e, f, :], start=(f == 0), stop=(f == FB - 1))
                        mm.then_inc(exp_mm, 1)

                    up(0)
                    for e in range(E):
                        if e + 1 < E:
                            up(e + 1)
                        if e == 0:
                            biases()
                        down(e)

        @block.scalar
        def _(act):
            def norm(inst):
                for p in range(NP):
                    act.wait_ge(ln_cen, inst * NP + p + 1)
                    nc.scalar.activation(piece(bbuf[1], p), piece(bbuf[0], p), ACT.Square).then_inc(ln_sq, 1)
                def log(p):
                    act.wait_ge(ln_var, inst * NP + p + 1)
                    nc.scalar.activation(piece(hbuf[0], p), ps[:, (7 + p % 3) % 8, 0:PW], ACT.Ln,
                                         bias=eps[:, 0:1]).then_inc(ln_log, 1)

                log(0)
                for p in range(NP):
                    if p + 1 < NP:
                        log(p + 1)
                    act.wait_ge(ln_log, inst * NP + p + 1)
                    nc.scalar.activation(piece(hbuf[0], p), piece(hbuf[0], p), ACT.Exp, scale=-0.5).then_inc(ln_rstd, 1)

            act.sem_inc(b_moved, 1)
            act.sem_inc(hid_done, 4)
            act.wait_ge(const_ld, 160)
            act.wait_ge(sel_made, 1)
            with act.Fori(0, HALVES) as hf:
                nc.scalar.preload_act_table_set("natural_log_exp_and_others")
                norm(hf * LN_PER_HALF)
                with act.Fori(0, LAYERS) as layer:
                    R = hf * LAYERS + layer

                    def silu(c, h):
                        act.wait_ge(conv_done, R * 4 + c * 2 + h + 1)
                        part_x = blk(xc, h)[:, c * CT:(c + 1) * CT]
                        nc.scalar.activation(part_x, part_x, ACT.Silu).then_inc(xc_ready, 1)

                    for q in range(4 * NP):
                        if q == 2 * NP:
                            nc.scalar.preload_act_table_set("silu_and_others")
                        if q == 4 * NP - 1:
                            silu(0, 0)
                        act.wait_ge(proj_mm, R * 4 * NP + q + 1)
                        dst = piece(blk(dtx, q // NP) if q < 2 * NP else blk(z, q // NP - 2), q % NP)
                        nc.scalar.activation(dst, ps[:, (q + 2) % 8, 0:PW], ACT.Copy if q < 2 * NP else ACT.Silu)\
                            .then_inc(proj_ev, 1)

                    def hi(p):
                        act.wait_ge(bc_mm, R * NP + p + 1)
                        nc.scalar.activation(piece(part[0], p), ps[:, bc_bank(p), 0:PW], ACT.Copy).then_inc(hi_done, 1)

                    def mid(p):
                        act.wait_ge(r1_done, R * NP + p + 1)
                        nc.scalar.activation(piece(part[1], p), piece(hbuf[0], p), ACT.Copy).then_inc(mid_done, 1)

                    def dt_abs_part(m):
                        h, p = DT_ORDER[m]
                        act.wait_ge(dt_mm, R * 2 * NP + m + 1)
                        nc.scalar.activation(piece(blk(dt, h), p), ps[:, dt_bank(m), 0:PW], ACT.Abs,
                                             bias=dt_b[:, h:h + 1]).then_inc(dt_abs, 1)

                    def dt_exp_part(c):
                        act.wait_ge(dt_abs, R * 2 * NP + (6 if c == 0 else 10))
                        nc.scalar.activation(chunk(dt, c), chunk(dt, c), ACT.Exp, scale=-1.0).then_inc(dt_exp, 1)

                    def dt_log_part(c):
                        act.wait_ge(dt_exp, R * 2 + c + 1)
                        for h in range(2):
                            side = blk(dt, h)[:, c * CT:(c + 1) * CT]
                            nc.scalar.activation(side, side, ACT.Ln, bias=eps[:, 1:2]).then_inc(dt_log, 1)

                    silu(0, 1)
                    hi(0)
                    hi(1)
                    dt_abs_part(0)
                    for h in range(2):
                        silu(1, h)
                    for m in range(1, 4):
                        dt_abs_part(m)
                    nc.scalar.preload_act_table_set("natural_log_exp_and_others")
                    nc.scalar.activation(nega[:], alog, ACT.Exp).then_inc(aexp_done, 1)
                    hi(2)
                    mid(0)
                    mid(1)
                    hi(3)
                    mid(2)
                    hi(4)
                    mid(3)
                    mid(4)
                    for m in range(4, 6):
                        dt_abs_part(m)
                    dt_exp_part(0)
                    dt_log_part(0)
                    for m in range(6, 10):
                        dt_abs_part(m)

                    def move_rows(i, v, p):
                        lo, hi = CUT[p]
                        act.wait_ge(b_spread, i * NC + p + 1)
                        nc.scalar.activation(bsp[v][:, lo:hi], ps[:, 5, 0:hi - lo], ACT.Copy).then_inc(b_moved, 1)

                    dt_exp_part(1)
                    act.wait_ge(scanned, R * 2 * NST + 1)
                    for p in range(NC):
                        move_rows(R * 2 * NST, 0, p)
                    dt_log_part(1)
                    act.wait_ge(nega_ready, R + 1)
                    for c in range(CHUNKS):
                        K = R * CHUNKS + c
                        act.wait_ge(dt_ready, K + 1)

                        def decay(jj, v, k):
                            h, n_im = k // 2, CI // 2
                            column = jj * 2 + (h * NST + (v % 2) * GSTEP + v // 2)
                            src = c * CI + k % 2 * n_im
                            return nc.scalar.activation(
                                images(abuf[v % 2][:])[:, k * n_im:(k + 1) * n_im, 1:SEQ],
                                images(blk(dt, h))[:, src:src + n_im, 1:SEQ],
                                ACT.Exp, scale=nega[:, ds(column, 1)])

                        def move_b(jj, v, first=False):
                            i = jj * 4 + v + K * NST
                            before = (jj, v - 1) if v else (jj - 1, 3)
                            act.wait_ge(scanned, i + 1)
                            for p in range(NC):
                                if not first:
                                    if p == 0:
                                        act.wait_ge(scanned, i + 2)
                                        decay(*before, 0)
                                    ins = decay(*before, p + 1)
                                    if p == 2:
                                        ins.then_inc(a_ready, 1)
                                move_rows(i, v, p)

                        if c:
                            move_b(0, 0, first=True)
                        for v in range(1, 4):
                            move_b(0, v)
                        with act.Fori(1, NST // 4) as jj:
                            for v in range(4):
                                move_b(jj, v)
                        act.wait_ge(scanned, (K + 1) * NST + 2)
                        for k in range(3):
                            decay(NST // 4 - 1, 3, k)
                        decay(NST // 4 - 1, 3, 3).then_inc(a_ready, 1)
                    norm(hf * LN_PER_HALF + 1 + layer)
                norm(hf * LN_PER_HALF + 1 + LAYERS)
                norm(hf * LN_PER_HALF + 2 + LAYERS)

                act.wait_ge(ln_out, (hf + 1) * LN_PER_HALF * NP)
                with act.Fori(0, AG // 2) as j:
                    def group(u):
                        return hf * AG + j * 2 + u

                    for u, w in enumerate(pair):
                        nc.scalar.activation(w.x, xs[:, ds((j * 2 + u) * AW, AW)], ACT.Copy).then_inc(att["hg"], 1)
                    for u, w in enumerate(pair):
                        act.wait_ge(att["qkv"], group(u) + 1)
                        nc.scalar.activation(w.sqk, ps[:, w.bank:w.bank + 2, 0:AW], ACT.Square)
                        nc.scalar.activation(w.v.rearrange("p b d -> p (b d)"), ps[0:SEQ, w.bank + 2, :], ACT.Copy)\
                            .then_inc(att["sq"], 1)
                    for u, w in enumerate(pair):
                        act.wait_ge(att["ssq"], group(u) + 1)
                        nc.scalar.activation(w.rqk, ps[:, w.bank + 2:w.bank + 4, 0:AW], ACT.Ln,
                                             bias=small[:, 0:1]).then_inc(att["log"], 1)
                    for u, w in enumerate(pair):
                        act.wait_ge(att["log"], group(u) + 1)
                        nc.scalar.activation(w.rqk, w.rqk, ACT.Exp, scale=-0.5).then_inc(att["r"], 1)
                    for u, w in enumerate(pair):
                        act.wait_ge(att["sub"], group(u) + 1)
                        nc.scalar.activation(w.sc, w.sc, ACT.Exp).then_inc(att["e"], 1)
                    for u, w in enumerate(pair):
                        act.wait_ge(att["t"], group(u) + 1)
                        nc.scalar.activation(w.pT.rearrange("p h b t -> p h (b t)"),
                                             ps[0:SEQ, w.bank + 2:w.bank + 4, 0:AW], ACT.Copy).then_inc(att["pt"], 1)
                    for u, w in enumerate(pair):
                        act.wait_ge(att["y"], group(u) + 1)
                        nc.scalar.activation(yT[:, ds((j * 2 + u) * AW, AW)], ps[:, w.bank + 1, 0:AW], ACT.Copy)\
                            .then_inc(att["yc"], 1)

                act.wait_ge(att["yc"], (hf + 1) * AG)
                with act.Fori(0, NP) as p:
                    q = hf * NP + p
                    nc.scalar.activation(yp, yT[:, ds(p * PW, PW)], ACT.Copy).then_inc(cp_done, 1)
                    nc.scalar.activation(hp, h0[:, ds(p * PW, PW)], ACT.Copy).then_inc(cp_done, 1)
                    nc.scalar.preload_act_table_set("natural_log_exp_and_others")
                    act.wait_ge(g_sub, q + 1)
                    nc.scalar.activation(gate, lg, ACT.Exp).then_inc(g_exp, 1)
                    nc.scalar.preload_act_table_set("gelu_apprx_tanh_and_others")
                    for e in range(E):
                        act.wait_ge(exp_mm, q * E + e + 1)
                        for f in range(FB):
                            act.wait_ge(hid_mm, q * E * FB + e * FB + f + 1)
                            nc.scalar.activation(hid[e % 2][:, f * PW:(f + 1) * PW], ps[:, f, 0:PW],
                                                 ACT.Gelu_apprx_tanh, bias=vffn[:, 4 + e * FB + f:5 + e * FB + f])\
                                .then_inc(hid_done, 1)

        @block.vector
        def _(dve):
            def norm(inst, source, dst, affine=None, g=None, b=None):
                for p in range(NP):
                    dve.wait_ge(ln_mean, inst * NP + p + 1)
                    nc.vector.tensor_tensor(piece(bbuf[0], p), piece(source, p), ps[:, 2 + p, 0:PW], ALU.subtract)\
                        .then_inc(ln_cen, 1)
                for p in range(NP):
                    dve.wait_ge(ln_rstd, inst * NP + p + 1)
                    if affine is None:
                        nc.vector.tensor_tensor(piece(dst, p), piece(bbuf[0], p), piece(hbuf[0], p), ALU.mult)\
                            .then_inc(ln_out, 1)
                    else:
                        nc.vector.tensor_tensor(piece(bbuf[0], p), piece(bbuf[0], p), piece(hbuf[0], p), ALU.mult)\
                            .then_inc(ln_nrm, 1)
                        dve.wait_ge(ln_nrm, affine * NP + p + 1)
                        nc.vector.tensor_scalar(piece(dst, p), piece(bbuf[0], p), g, b, ALU.mult, ALU.add)\
                            .then_inc(ln_out, 1)

            dve.sem_inc(tok_mm, 2)
            dve.sem_inc(tok_ev, 2)
            dve.sem_inc(g_ready, 2)
            dve.sem_inc(scanned, 4)
            dve.sem_inc(y_gated, 1)
            dve.sem_inc(exp_added, 2)
            dve.sem_inc(piece_done, 1)
            for u in range(2):
                nc.vector.memset(images(abuf[u][:])[:, :, 0:1], 0.0)
            nc.vector.memset(eps[:, 0:1], EPS)
            nc.vector.memset(eps[:, 1:2], 1.0)
            nc.vector.memset(small[:, 0:1], 1e-12)
            dve.wait_ge(const_ld, 160)
            nc.vector.tensor_scalar(kg8[:], vffn[:, 3:4], float(DH) ** 0.5, None, ALU.mult).then_inc(kg_done, 1)
            nc.vector.tensor_copy(sel[:], eye32[:].unsqueeze(2).broadcast_to([96, GSTEP, 128])).then_inc(sel_made, 1)
            with dve.Fori(0, HALVES) as hf:
                nc.vector.tensor_scalar(images(h0[:])[:, :, 0], vtok[:, 1:2].broadcast_to([128, HB]), posT[:, 0:1],
                                        None, ALU.mult).then_inc(cls_done, 1)
                with dve.Fori(0, TOKG // 2) as j:
                    for u in range(2):
                        dve.wait_ge(tok_mm, hf * (TOKG + 2) + j * 2 + u + 3)
                        dst = images(h0[:, ds((j * 2 + u) * TOKB * SEQ, TOKB * SEQ)])[:, :, 1:SEQ]
                        nc.vector.scalar_tensor_tensor(
                            out=dst, in0=ps[:, u, 0:TOKB * 64].rearrange("p (b t) -> p b t", b=TOKB),
                            scalar=vtok[:, 0:1], in1=posT[:, 1:SEQ].unsqueeze(1).broadcast_to([128, TOKB, 64]),
                            op0=ALU.add, op1=ALU.mult).then_inc(tok_ev, 1)
                norm(hf * LN_PER_HALF, h0, xs)

                with dve.Fori(0, LAYERS) as layer:
                    R = hf * LAYERS + layer
                    dve.wait_ge(w_ld, R * 64 + 64)
                    for c in range(CHUNKS):
                        side = slice(c * CT, (c + 1) * CT)
                        done = (R * CHUNKS + c) * 2 * TAPS
                        order = [(0, 0), (1, 0), (0, 1), (2, 0), (1, 1), (3, 0), (2, 1), (3, 1)]
                        for k, (s, h) in enumerate(order):
                            raw, conv = blk(dtx, h)[:, side], blk(xc, h)[:, side]
                            if s == 0:
                                dve.wait_ge(proj_ev, R * 4 * NP + h * NP + (3 if c == 0 else NP))
                                nc.vector.tensor_scalar(conv, raw, conv_w[:, h, TAPS - 1:TAPS],
                                                        conv_b[:, h:h + 1], ALU.mult, ALU.add).then_inc(conv_step, 1)
                                continue
                            dve.wait_ge(conv_step, done + order.index((s - 1, h)) + 1)
                            now = images(conv)[:, :, s:SEQ]
                            nc.vector.scalar_tensor_tensor(
                                out=now, in0=images(raw)[:, :, 0:SEQ - s],
                                scalar=conv_w[:, h, TAPS - 1 - s:TAPS - s], in1=now, op0=ALU.mult,
                                op1=ALU.add).then_inc(conv_step, 1)
                            if (s, h) == (TAPS - 1, 0):
                                dve.wait_ge(conv_step, done + k + 1)
                                dve.sem_inc(conv_done, 1)
                        dve.wait_ge(conv_step, done + 2 * TAPS)
                        dve.sem_inc(conv_done, 1)

                    def rest(p):
                        dve.wait_ge(hi_done, R * NP + p + 1)
                        nc.vector.tensor_tensor(piece(hbuf[0], p), ps[:, bc_bank(p), 0:PW], piece(part[0], p),
                                                ALU.subtract).then_inc(r1_done, 1)

                    def low(p):
                        dve.wait_ge(mid_done, R * NP + p + 1)
                        nc.vector.tensor_tensor(piece(part[2], p), piece(hbuf[0], p), piece(part[1], p),
                                                ALU.subtract).then_inc(lo_done, 1)

                    def relu_part(m):
                        h, p = DT_ORDER[m]
                        dve.wait_ge(dt_abs, R * 2 * NP + m + 1)
                        nc.vector.tensor_scalar(piece(blk(dtx, h), p), ps[:, dt_bank(m), 0:PW],
                                                dt_b[:, h:h + 1], 0.0, ALU.add, ALU.max).then_inc(dt_relu, 1)

                    def dt_sum(c):
                        dve.wait_ge(dt_relu, R * 2 * NP + (6 if c == 0 else 10))
                        for h in range(2):
                            dve.wait_ge(dt_log, (R * 2 + c) * 2 + h + 1)
                            side, more = (blk(a, h)[:, c * CT:(c + 1) * CT] for a in (dt, dtx))
                            ins = nc.vector.tensor_tensor(side, side, more, ALU.add)
                        ins.then_inc(dt_ready, 1)

                    def dt_times_x(c):
                        dve.wait_ge(dt_ready, R * 2 + c + 1)
                        nc.vector.tensor_tensor(chunk(dtx, c), chunk(dt, c), chunk(xc, c), ALU.mult)\
                            .then_inc(dtx_ready, 1)

                    for h in range(2):
                        ins = nc.vector.tensor_scalar(dskip[:, h, :], ident, dvec[:, h:h + 1], None, ALU.mult)
                    ins.then_inc(dskip_ready, 1)
                    rest(0)
                    rest(1)
                    for m in range(4):
                        relu_part(m)
                    dve.wait_ge(aexp_done, R + 1)
                    nc.vector.tensor_scalar(nega[:], nega[:], -1.0, None, ALU.mult).then_inc(nega_ready, 1)
                    rest(2)
                    low(0)
                    low(1)
                    rest(3)
                    low(2)
                    rest(4)
                    low(3)
                    low(4)
                    for m in range(4, 6):
                        relu_part(m)
                    dt_sum(0)
                    dt_times_x(0)
                    for m in range(6, 10):
                        relu_part(m)
                    dt_sum(1)
                    dt_times_x(1)
                    def gate_sums(c):
                        K = R * CHUNKS + c
                        for k, (lo, hi) in enumerate(CUT):
                            if k < 2:
                                dve.wait_ge(y_sum, K * 2 + k + 1)
                            else:
                                dve.wait_ge(y_added, (K + 1) * NST + 4)
                            zz = both(z)[:, :, c * CT + lo:c * CT + hi]
                            yy = ps[:, 2 * k:2 * k + 2, 0:PW] if k < 2 else both(ps[:, 4, 0:PW])
                            ins = nc.vector.tensor_tensor(zz, zz, yy, ALU.mult)
                        ins.then_inc(y_gated, 1)

                    for c in range(CHUNKS):
                        K = R * CHUNKS + c

                        def weigh(i, v):
                            dve.wait_ge(scanned, i + 5)
                            for p, (lo, hi) in enumerate(CUT):
                                dve.wait_ge(c_spread, i * NC + p + 1)
                                hh = both(hbuf[v][:])[:, :, lo:hi]
                                cc = ps[:, 6 + (v + p) % 2, 0:hi - lo].unsqueeze(1).broadcast_to([128, 2, hi - lo])
                                nc.vector.tensor_tensor(hh, hh, cc, ALU.mult).then_inc(g_ready, 1)

                        def step(jj, v, first=False):
                            i = jj * 4 + v + K * NST
                            dve.wait_ge(a_ready, i + 1)
                            dve.wait_ge(b_ready, i + 1)
                            dve.wait_ge(y_added, i + 1)
                            nc.vector.tensor_tensor_scan(hbuf[v][:], abuf[v % 2][:], bbuf[v % 2][:], 0.0, ALU.mult,
                                                         ALU.add).then_inc(scanned, 1)
                            if not first:
                                weigh(i - 1, (v - 1) % 4)

                        step(0, 0, first=True)
                        if c:
                            gate_sums(c - 1)
                        for v in range(1, 4):
                            step(0, v)
                        with dve.Fori(0, (NST // 4 - 1) // 3) as t:
                            for k in range(3):
                                for v in range(4):
                                    step(t * 3 + k + 1, v)
                        weigh(K * NST + NST - 1, 3)
                    gate_sums(CHUNKS - 1)
                    for p in range(NP):
                        dve.wait_ge(o_mm, R * NP + p + 1)
                        nc.vector.tensor_tensor(piece(hbuf[1], p), piece(xs, p), ps[:, (5 + p) % 8, 0:PW], ALU.add)\
                            .then_inc(o_res, 1)
                    dve.wait_ge(o_ld, R * 32 + 32)
                    norm(hf * LN_PER_HALF + 1 + layer, hbuf[1], xs, hf * (LAYERS + 1) + layer, ln_g, ln_b)
                    dve.wait_ge(ln_out, (hf * LN_PER_HALF + 2 + layer) * NP)
                    dve.sem_inc(ln_used, 1)

                nc.vector.tensor_tensor(h0[:], h0[:], xs[:], ALU.add).then_inc(h1_ready, 1)
                norm(hf * LN_PER_HALF + 1 + LAYERS, h0, xs)
                norm(hf * LN_PER_HALF + 2 + LAYERS, xs, xs, hf * (LAYERS + 1) + LAYERS, vffn[:, 0:1], vffn[:, 1:2])

                with dve.Fori(0, AG // 2) as j:
                    def group(u):
                        return hf * AG + j * 2 + u

                    def soft(k, u):
                        return (hf * AG // 2 + j) * 8 + k * 2 + u + 1

                    def rows3(w):
                        return w.sc.rearrange("p (k t) -> p k t", t=SEQ)

                    def per_row(a):
                        return a.unsqueeze(2).broadcast_to([SEQ, HEADS * AB, SEQ])

                    dve.wait_ge(kg_done, 1)
                    for u, w in enumerate(pair):
                        dve.wait_ge(att["r"], group(u) + 1)
                        nc.vector.scalar_tensor_tensor(out=w.qn, in0=ps[:, w.bank, 0:AW], scalar=vffn[:, 2:3],
                                                       in1=w.rqk[:, 0, :], op0=ALU.mult, op1=ALU.mult)
                        nc.vector.scalar_tensor_tensor(out=w.kn, in0=ps[:, w.bank + 1, 0:AW], scalar=kg8[:, 0:1],
                                                       in1=w.rqk[:, 1, :], op0=ALU.mult, op1=ALU.mult)\
                            .then_inc(att["n"], 1)
                    for u, w in enumerate(pair):
                        dve.wait_ge(att["s"], group(u) + 1)
                        s4 = w.sc.rearrange("p (h b t) -> p h b t", h=HEADS, b=AB)
                        for h in range(HEADS):
                            ins = nc.vector.tensor_tensor(
                                s4[:, h], ps[0:SEQ, w.bank + h, 0:AW].rearrange("p (b t) -> p b t", b=AB),
                                msk[:].unsqueeze(1).broadcast_to([SEQ, AB, SEQ]), ALU.add)
                        ins.then_inc(att["soft"], 1)
                    for u, w in enumerate(pair):
                        dve.wait_ge(att["soft"], soft(0, u))
                        nc.vector.tensor_reduce(w.mx, rows3(w), AX_X, ALU.max).then_inc(att["soft"], 1)
                    for u, w in enumerate(pair):
                        dve.wait_ge(att["soft"], soft(1, u))
                        nc.vector.tensor_tensor(rows3(w), rows3(w), per_row(w.mx), ALU.subtract)\
                            .then_inc(att["sub"], 1)
                    for u, w in enumerate(pair):
                        dve.wait_ge(att["e"], group(u) + 1)
                        nc.vector.tensor_reduce(w.rs, rows3(w), AX_X, ALU.add).then_inc(att["soft"], 1)
                    for u, w in enumerate(pair):
                        dve.wait_ge(att["soft"], soft(2, u))
                        nc.vector.reciprocal(w.rs, w.rs).then_inc(att["soft"], 1)
                    for u, w in enumerate(pair):
                        dve.wait_ge(att["soft"], soft(3, u))
                        nc.vector.tensor_tensor(rows3(w), rows3(w), per_row(w.rs), ALU.mult).then_inc(att["p"], 1)
                    for u, w in enumerate(pair):
                        dve.wait_ge(att["o"], group(u) + 1)
                        nc.vector.tensor_copy(w.o, ps[:, w.bank, 0:AW]).then_inc(att["oc"], 1)

                g3 = gate.rearrange("p (t e) -> p t e", t=MB)
                l3 = lg.rearrange("p (t e) -> p t e", t=MB)
                gm, gs = small[0:MT, 48:52], small[0:MT, 52:56]
                with dve.Fori(0, NP) as p:
                    q = hf * NP + p
                    dve.wait_ge(gate_mm, q + 1)
                    pg = ps[0:MT, 6, 0:MB * E].rearrange("p (t e) -> p t e", t=MB)
                    nc.vector.tensor_reduce(gm, pg, AX_X, ALU.max).then_inc(g_soft, 1)
                    dve.wait_ge(g_soft, q * 4 + 1)
                    nc.vector.tensor_tensor(l3, pg, gm.unsqueeze(2).broadcast_to([MT, MB, E]), ALU.subtract)\
                        .then_inc(g_sub, 1)
                    dve.wait_ge(g_exp, q + 1)
                    nc.vector.tensor_reduce(gs, g3, AX_X, ALU.add).then_inc(g_soft, 1)
                    dve.wait_ge(g_soft, q * 4 + 2)
                    nc.vector.reciprocal(gs, gs).then_inc(g_soft, 1)
                    dve.wait_ge(g_soft, q * 4 + 3)
                    nc.vector.tensor_tensor(g3, g3, gs.unsqueeze(2).broadcast_to([MT, MB, E]), ALU.mult)\
                        .then_inc(g_soft, 1)
                    dve.wait_ge(gt_mm, q + 1)
                    nc.vector.tensor_copy(gate_t, ps[0:E, 6, 0:PW]).then_inc(gt_done, 1)
                    dve.wait_ge(out_st, q * 16 + 16)
                    dve.wait_ge(tr_mm, q + 1)
                    nc.vector.tensor_copy(acc, ps[0:MT, 7, :]).then_inc(acc_step, 1)
                    for e in range(E):
                        dve.wait_ge(exp_mm, q * E + e + 3)
                        for t in range(MB):
                            dve.wait_ge(acc_step, q * (E * MB + 1) + 1 + ((e - 1) * MB + t + 1 if e else 0))
                            nc.vector.scalar_tensor_tensor(
                                out=acc[:, t * D:(t + 1) * D], in0=ps[0:MT, 4 + e % 2, t * D:(t + 1) * D],
                                scalar=gate[:, t * E + e:t * E + e + 1], in1=acc[:, t * D:(t + 1) * D],
                                op0=ALU.mult, op1=ALU.add).then_inc(acc_step, 1)
                        dve.wait_ge(acc_step, q * (E * MB + 1) + 1 + (e + 1) * MB)
                        dve.sem_inc(exp_added, 1)
                    dve.sem_inc(piece_done, 1)
                dve.sem_inc(tok_mm, 2)

        @block.gpsimd
        def _(pool):
            with pool.Fori(0, HALVES * LAYERS) as R:
                for c in range(CHUNKS):
                    K = R * CHUNKS + c
                    x_dt = chunk(dtx, c)
                    with pool.Fori(0, NST // 16) as t:
                        for k in range(16):
                            v = k % 4
                            i = K * NST + t * 16 + k
                            pool.wait_ge(dtx_ready, K + 1)
                            pool.wait_ge(scanned, i + 3)
                            pool.wait_ge(b_moved, i * NC + NC + 1)
                            nc.gpsimd.tensor_tensor(both(bbuf[v % 2][:]),
                                                    bsp[v][:].unsqueeze(1).broadcast_to([128, 2, CT]),
                                                    x_dt, ALU.mult).then_inc(b_ready, 1)


def kernel(**inputs):
    import concourse.bacc as bacc
    from concourse.bass_utils import run_bass_kernel_spmd as run

    a = {k: np.asarray(v) for k, v in inputs.items()}

    def chan(v, n):
        return np.swapaxes(v.reshape(v.shape[0], n, 128, *v.shape[2:]), 1, 2)

    def attn(n):
        return a["L0_attn_" + n]

    def ring(v):
        return np.concatenate([v, v[:1]], axis=0)

    def ffn(n):
        return a["L0_ffn_" + n]

    par = np.concatenate([
        chan(attn("conv_w")[:, :, 0, :], 2).reshape(LAYERS, 128, 2 * TAPS),
        chan(attn("conv_b"), 2), chan(attn("dt_b"), 2), chan(attn("D_param"), 2),
        chan(attn("A_log"), 2).reshape(LAYERS, 128, 2 * NST)], axis=2)
    par_ln = np.stack([attn("ln_g"), attn("ln_b")], axis=2)
    v_ffn = np.concatenate([
        ffn("ln_g")[:, None], ffn("ln_b")[:, None], np.concatenate([ffn("qn_g")] * HEADS)[:, None],
        np.concatenate([ffn("kn_g")] * HEADS)[:, None], ffn("b1").reshape(E * FB, 128).T], axis=1)
    ones = np.ones((128,), np.float32)
    r_ffn = np.concatenate([ffn("gate_b"), ones])[None, :]
    head = np.arange(128) // DH
    consts = np.concatenate([np.eye(128), np.full((128, 128), 1.0 / D), head[:, None] == head[None, :]],
                            axis=1).astype(np.float32)
    onehot = np.concatenate([np.eye(GSTEP)] * 3, axis=0).astype(np.float32)
    mask = np.where(np.tril(np.ones((SEQ, SEQ), bool)), 0.0, -3e38).astype(np.float32)
    arrays = {
        "x": a["x"].reshape(B // TOKB, TOKB, C, GRID, PATCH, GRID, PATCH).transpose(2, 4, 6, 0, 1, 3, 5)
        .reshape(KT, ROWS, B // TOKB, TOKB * 64).transpose(1, 2, 0, 3).reshape(ROWS, B // TOKB * TOKE),
        "w_tok": a["L0_tok_W"].reshape(D, KT, ROWS).transpose(2, 1, 0).reshape(ROWS, KT * D),
        "v_tok": np.stack([a["L0_tok_b"], a["L0_tok_class_token"][0]], axis=1),
        "pos": a["L0_tok_pos_embed"].T,
        "w_in": ring(attn("in_proj_w")), "w_x": ring(attn("x_proj_w")), "w_dt": ring(attn("dt_w")),
        "w_out": ring(attn("out_w")), "par": ring(par), "par_ln": ring(par_ln),
        "w_att": np.concatenate([ffn("Wq"), ffn("Wk"), ffn("Wv"), ffn("Wo")], axis=1),
        "w_gate": ffn("gate_W"), "v_ffn": v_ffn, "r_ffn": r_ffn, "w_b2": ffn("b2"),
        "w1": ffn("W1").transpose(1, 0, 2).reshape(D, E * FF),
        "w2": ffn("W2").reshape(E, FB, 128, D).transpose(2, 0, 1, 3).reshape(128, E * FB * D),
        "consts": consts, "onehot": onehot, "mask": mask,
    }
    nc = bacc.Bacc("TRN2", target_bir_lowering=False, num_devices=1)
    fed, args = {}, []
    for name, v in arrays.items():
        v = np.ascontiguousarray(v)
        fed["in_" + name] = v
        args.append(nc.dram_tensor("in_" + name, v.shape, mybir.dt.from_np(v.dtype), kind="ExternalInput").ap())
    result = nc.dram_tensor("out", (B * SEQ, D), F32, kind="ExternalOutput").ap()
    bass_vit_tower(nc, *args, result)
    r = run(nc, [fed], core_ids=[0])
    return r.results[0]["out"].reshape(B, SEQ, D)
```
